# Optimizing a Trainium2 kernel written in Bass

```python
import numpy as np
import jax
import jax.numpy as jnp

def _softmax(x, axis=-1):
    return jax.nn.softmax(x, axis=axis)

def _gelu(x):
    return jax.nn.gelu(x, approximate=True)

def _silu(x):
    return jax.nn.silu(x)

def _sigmoid(x):
    return jax.nn.sigmoid(x)

def _layernorm(x, axis=-1, eps=1e-05):
    m = jnp.mean(x, axis=axis, keepdims=True)
    v = jnp.var(x, axis=axis, keepdims=True)
    return (x - m) / jnp.sqrt(v + eps)

def _scatter_add(tgt, idx, src, axis=0):
    return tgt.at[idx].add(src)

def _segment_sum(src, seg, n):
    return jax.ops.segment_sum(src, seg, n)
kernel_name = 'mk_flamingo_gated_d4_seqx_r8_ba817b'

def setup_inputs(seed: int=0):
    np.random.seed(seed)
    _w = jnp.asarray

    def _rec_inputs():
        import jax
        import jax.numpy as jnp
        _rk = jax.random.key(seed)
        x = -0.0002928 + 1 * jax.random.normal(jax.random.fold_in(_rk, 1), (8, 256, 128), jnp.float32)
        _lenS = 256 - jax.random.randint(jax.random.fold_in(_rk, 7), (8,), 0, max(1, 256 // 4) + 1, jnp.int32)
        _lenS2 = 256 - jax.random.randint(jax.random.fold_in(_rk, 8), (8,), 0, max(1, 256 // 4) + 1, jnp.int32)
        _ctx_1024P = jax.random.normal(jax.random.fold_in(_rk, 11), (8, 16, 128), jnp.float32)
        _ctx_1024c = jax.random.dirichlet(jax.random.fold_in(_rk, 511), 0.3 * jnp.ones((16,), jnp.float32), (8, 256))
        _ctx_1024t = jnp.einsum('bsk,bkd->bsd', _ctx_1024c, _ctx_1024P)
        _ctx_1024t = _ctx_1024t * jax.lax.rsqrt(jnp.mean(jnp.square(_ctx_1024t)) + 1e-12) * 0.953939
        ctx_1024 = -1.39393e-06 + 0.999914 * (_ctx_1024t + 0.3 * jax.random.normal(jax.random.fold_in(_rk, 611), (8, 256, 128), jnp.float32))
        _validS = jnp.arange(256)[None, :] < _lenS[:, None]
        _validS2 = jnp.arange(256)[None, :] < _lenS2[:, None]
        _causal = jnp.tril(jnp.ones((256, 256), dtype=bool))
        mask_BxSxS2_ik1 = jnp.where(jnp.broadcast_to(_validS2[:, None, :], (8, 256, 256)), 1, 0).astype(jnp.int32)
        mask_Bx1xSxS2_bk1 = jnp.broadcast_to(_validS2[:, None, None, :], (8, 1, 256, 256))
        _g = jax.random.normal(jax.random.fold_in(_rk, 9001), (2, 4), jnp.float32)
        _g = jnp.sign(_g) * jnp.maximum(jnp.abs(_g), 1.0) + (_g == 0) * 1.0
        g_xattn = _g[0]
        g_ffn = _g[1]
        return (x, ctx_1024, mask_BxSxS2_ik1, mask_Bx1xSxS2_bk1, g_xattn, g_ffn)
    x, ctx_1024, mask_BxSxS2_ik1, mask_Bx1xSxS2_bk1, g_xattn, g_ffn = _rec_inputs()

    def _L0_xattn_setup():
        import jax, jax.numpy as jnp
        import numpy as np
        B, S, E, H = (2, 256, 128, 16)
        D = E // H
        key = jax.random.key(seed)
        ks = jax.random.split(key, 7)
        scale = 0.02
        return {'inputs': jax.random.normal(ks[0], (B, S, E), jnp.float32), 'embbeding_V': jax.random.normal(ks[1], (B, S, E), jnp.float32), 'embbeding_K': jax.random.normal(ks[2], (B, S, E), jnp.float32), 'Wq': jax.random.normal(ks[3], (E, E), jnp.float32) * scale, 'Wk': jax.random.normal(ks[4], (E, E), jnp.float32) * scale, 'Wv': jax.random.normal(ks[5], (E, E), jnp.float32) * scale, 'Wo': jax.random.normal(ks[6], (E, E), jnp.float32) * scale}
    _L0_xattn_all = _L0_xattn_setup()
    _L0_xattn_in = {k: v for k, v in _L0_xattn_all.items() if k in ('Wq', 'Wk', 'Wv', 'Wo')}
    del _L0_xattn_all

    def _L0_ffn_setup():
        import jax, jax.numpy as jnp
        import numpy as np
        EPS = 1e-12

        def _l2norm(v):
            n = jnp.sqrt(jnp.sum(v * v, axis=-1, keepdims=True))
            return v / jnp.maximum(n, EPS)
        key = jax.random.key(seed)
        ks = jax.random.split(key, 6)
        B, S, D, F, E = (2, 256, 128, 512, 8)
        std = 0.02
        return {'x': jax.random.normal(ks[0], (B, S, D), jnp.float32), 'Wp': jax.random.normal(ks[1], (D, D), jnp.float32) * (1.0 / np.sqrt(D)), 'sim_matrix': jax.random.normal(ks[2], (E, D), jnp.float32) * std, 'temperature': jnp.asarray(1.0, jnp.float32), 'W1': jax.random.normal(ks[3], (E, D, F), jnp.float32) * (1.0 / np.sqrt(D)), 'b1': jnp.zeros((E, F), jnp.float32), 'W2': jax.random.normal(ks[4], (E, F, D), jnp.float32) * (1.0 / np.sqrt(F)), 'b2': jnp.zeros((E, D), jnp.float32)}
    _L0_ffn_all = _L0_ffn_setup()
    _L0_ffn_in = {k: v for k, v in _L0_ffn_all.items() if k in ('Wp', 'sim_matrix', 'temperature', 'W1', 'b1', 'W2', 'b2')}
    del _L0_ffn_all

    def _L1_xattn_setup():
        import jax, jax.numpy as jnp
        import numpy as np
        B, S, D, H = (2, 256, 128, 16)
        DK = D // H
        key = jax.random.key(seed)
        ks = jax.random.split(key, 8)
        return {'query': jax.random.normal(ks[0], (B, S, D), dtype=jnp.float32), 'key': jax.random.normal(ks[1], (B, S, D), dtype=jnp.float32), 'value': jax.random.normal(ks[2], (B, S, D), dtype=jnp.float32), 'mask': jax.random.randint(ks[3], (B, S, S), 0, 2, dtype=jnp.int32), 'w_q': jax.random.normal(ks[4], (D, D), dtype=jnp.float32) * D ** (-0.5), 'w_k': jax.random.normal(ks[5], (D, D), dtype=jnp.float32) * D ** (-0.5), 'w_v': jax.random.normal(ks[6], (D, D), dtype=jnp.float32) * D ** (-0.5), 'w_o': jax.random.normal(ks[7], (D, D), dtype=jnp.float32) * D ** (-0.5)}
    _L1_xattn_all = _L1_xattn_setup()
    _L1_xattn_in = {k: v for k, v in _L1_xattn_all.items() if k in ('w_q', 'w_k', 'w_v', 'w_o')}
    del _L1_xattn_all

    def _L1_ffn_setup():
        import jax, jax.numpy as jnp
        import numpy as np

        def _bitlinear(x, w_latent):
            scale = jax.lax.stop_gradient(jnp.clip(jnp.mean(jnp.abs(w_latent), axis=1, keepdims=True), 1e-05, None))
            tern = jnp.clip(jnp.round(w_latent / scale), -1.0, 1.0)
            w = w_latent + jax.lax.stop_gradient(tern - w_latent)
            return x @ (w * scale).T
        key = jax.random.key(seed)
        ks = jax.random.split(key, 6)
        dim, hidden, rank = (128, 512, 16)
        B, S = (4, 512)
        x = jax.random.normal(ks[0], (B, S, dim), dtype=jnp.float32)
        w_fc = 0.02 * jax.random.normal(ks[1], (hidden, dim), dtype=jnp.float32)
        w_proj = 0.02 * jax.random.normal(ks[2], (dim, hidden), dtype=jnp.float32)
        u = 0.02 * jax.random.normal(ks[3], (hidden, rank), dtype=jnp.float32)
        v = 0.02 * jax.random.normal(ks[4], (rank, dim), dtype=jnp.float32)
        fast_b = jax.random.normal(ks[5], (rank, rank), dtype=jnp.float32)
        gate = jnp.float32(0.05)
        return {'x': x, 'fast_b': fast_b, 'w_fc': w_fc, 'w_proj': w_proj, 'u': u, 'v': v, 'gate': gate}
    _L1_ffn_all = _L1_ffn_setup()
    _L1_ffn_in = {k: v for k, v in _L1_ffn_all.items() if k in ('fast_b', 'w_fc', 'w_proj', 'u', 'v', 'gate')}
    del _L1_ffn_all

    def _L2_xattn_setup():
        import jax, jax.numpy as jnp
        import numpy as np
        H, DK, DV = (16, 64, 64)
        MEM = 128
        D_MODEL = 128
        OUT_DIM = 128
        key = jax.random.key(seed)
        ks = jax.random.split(key, 12)
        B, S = (2, 256)
        scale = 1.0 / np.sqrt(D_MODEL)
        inp = {'queries': jax.random.normal(ks[0], (B, S, D_MODEL), jnp.float32), 'keys': jax.random.normal(ks[1], (B, S, D_MODEL), jnp.float32), 'values': jax.random.normal(ks[2], (B, S, D_MODEL), jnp.float32), 'wq_w': jax.random.normal(ks[3], (D_MODEL, H * DK), jnp.float32) * scale, 'wq_b': jnp.zeros((H * DK,), jnp.float32), 'wk_w': jax.random.normal(ks[4], (D_MODEL, H * DK), jnp.float32) * scale, 'wk_b': jnp.zeros((H * DK,), jnp.float32), 'wv_w': jax.random.normal(ks[5], (D_MODEL, H * DV), jnp.float32) * scale, 'wv_b': jnp.zeros((H * DV,), jnp.float32), 'mk': jax.random.normal(ks[6], (1, MEM, H * DK), jnp.float32) * (0.1 / DK), 'mv': jax.random.normal(ks[7], (1, MEM, H * DV), jnp.float32) * (0.1 / MEM), 'wo_w': jax.random.normal(ks[8], (H * DV, OUT_DIM), jnp.float32) * (1.0 / np.sqrt(H * DV)), 'wo_b': jnp.zeros((OUT_DIM,), jnp.float32)}
        return inp
    _L2_xattn_all = _L2_xattn_setup()
    _L2_xattn_in = {k: v for k, v in _L2_xattn_all.items() if k in ('wq_w', 'wq_b', 'wk_w', 'wk_b', 'wv_w', 'wv_b', 'mk', 'mv', 'wo_w', 'wo_b')}
    del _L2_xattn_all

    def _L2_ffn_setup():
        import jax, jax.numpy as jnp
        import numpy as np
        TEMPERATURE = 1.0
        TOPK = 2
        key = jax.random.key(seed)
        ks = jax.random.split(key, 6)
        S, B, H, F, E = (256, 4, 128, 512, 8)
        x = jax.random.normal(ks[0], (S, B, H), dtype=jnp.float32)
        gate_w = jax.random.normal(ks[1], (E, H), dtype=jnp.float32) * (1.0 / np.sqrt(H))
        w1 = jax.random.normal(ks[2], (E, H, F), dtype=jnp.float32) * (1.0 / np.sqrt(H))
        b1 = jnp.zeros((E, F), dtype=jnp.float32)
        w2 = jax.random.normal(ks[3], (E, F, H), dtype=jnp.float32) * (1.0 / np.sqrt(F))
        b2 = jnp.zeros((E, H), dtype=jnp.float32)
        return {'x': x, 'gate_w': gate_w, 'w1': w1, 'b1': b1, 'w2': w2, 'b2': b2}
    _L2_ffn_all = _L2_ffn_setup()
    _L2_ffn_in = {k: v for k, v in _L2_ffn_all.items() if k in ('gate_w', 'w1', 'b1', 'w2', 'b2')}
    del _L2_ffn_all

    def _L3_xattn_setup():
        import jax, jax.numpy as jnp
        import numpy as np
        B, S, D, H = (4, 256, 128, 16)
        HD = D // H
        key = jax.random.key(seed)
        ks = jax.random.split(key, 12)
        scale = 1.0 / np.sqrt(D)
        inp = {'queries': jax.random.normal(ks[0], (B, S, D), jnp.float32), 'keys': jax.random.normal(ks[1], (B, S, D), jnp.float32), 'values': jax.random.normal(ks[2], (B, S, D), jnp.float32), 'mask': jax.random.randint(ks[3], (B, 1, S, S), 0, 2).astype(bool), 'Wq': jax.random.normal(ks[4], (D, D), jnp.float32) * scale, 'bq': jnp.zeros((D,), jnp.float32), 'Wk': jax.random.normal(ks[5], (D, D), jnp.float32) * scale, 'bk': jnp.zeros((D,), jnp.float32), 'Wv': jax.random.normal(ks[6], (D, D), jnp.float32) * scale, 'bv': jnp.zeros((D,), jnp.float32), 'Wo': jax.random.normal(ks[7], (D, D), jnp.float32) * scale, 'bo': jnp.zeros((D,), jnp.float32)}
        return inp
    _L3_xattn_all = _L3_xattn_setup()
    _L3_xattn_in = {k: v for k, v in _L3_xattn_all.items() if k in ('Wq', 'bq', 'Wk', 'bk', 'Wv', 'bv', 'Wo', 'bo')}
    del _L3_xattn_all

    def _L3_ffn_setup():
        import jax, jax.numpy as jnp
        import numpy as np
        EMB = 128
        HID = 256
        HEADS = 16
        HEAD_DIM = EMB // HEADS
        EXPERTS = 8
        TOPK = 2
        EPS = 1e-05

        def layernorm(x, scale, shift):
            mean = jnp.mean(x, axis=-1, keepdims=True)
            var = jnp.mean((x - mean) ** 2, axis=-1, keepdims=True)
            return scale * (x - mean) / jnp.sqrt(var + EPS) + shift

        def attention(x, wq, wk, wv, wo, bo):
            b, t, _ = x.shape
            q = (x @ wq).reshape(b, t, HEADS, HEAD_DIM)
            k = (x @ wk).reshape(b, t, HEADS, HEAD_DIM)
            v = (x @ wv).reshape(b, t, HEADS, HEAD_DIM)
            scores = jnp.einsum('bqhd,bkhd->bhqk', q, k)
            mask = jnp.arange(t)[:, None] < jnp.arange(t)[None, :]
            scores = jnp.where(mask, -jnp.inf, scores)
            attn = jax.nn.softmax(scores / np.sqrt(HEAD_DIM), axis=-1)
            ctx = jnp.einsum('bhqk,bkhd->bqhd', attn, v).reshape(b, t, EMB)
            return ctx @ wo + bo

        def moe_ff(x, gate_w, w1, w2, w3):
            b, t, d = x.shape
            xf = x.reshape(b * t, d)
            scores = xf @ gate_w
            topk_scores, topk_idx = jax.lax.top_k(scores, TOPK)
            topk_probs = jax.nn.softmax(topk_scores, axis=-1)
            weight = jnp.sum(jax.nn.one_hot(topk_idx, EXPERTS, dtype=xf.dtype) * topk_probs[..., None], axis=1)
            h = jax.nn.silu(jnp.einsum('td,edh->eth', xf, w1)) * jnp.einsum('td,edh->eth', xf, w2)
            out_e = jnp.einsum('eth,ehd->etd', h, w3)
            out = jnp.einsum('etd,te->td', out_e, weight)
            return out.reshape(b, t, d)
        key = jax.random.key(seed)
        ks = jax.random.split(key, 12)
        s = lambda k, shape, fan: jax.random.normal(k, shape, jnp.float32) / np.sqrt(fan)
        return {'x': jax.random.normal(ks[0], (2, 256, EMB), jnp.float32), 'ln1_scale': jnp.ones((EMB,), jnp.float32), 'ln1_shift': jnp.zeros((EMB,), jnp.float32), 'wq': s(ks[1], (EMB, EMB), EMB), 'wk': s(ks[2], (EMB, EMB), EMB), 'wv': s(ks[3], (EMB, EMB), EMB), 'wo': s(ks[4], (EMB, EMB), EMB), 'bo': jnp.zeros((EMB,), jnp.float32), 'ln2_scale': jnp.ones((EMB,), jnp.float32), 'ln2_shift': jnp.zeros((EMB,), jnp.float32), 'gate_w': s(ks[5], (EMB, EXPERTS), EMB), 'w1': s(ks[6], (EXPERTS, EMB, HID), EMB), 'w2': s(ks[7], (EXPERTS, EMB, HID), EMB), 'w3': s(ks[8], (EXPERTS, HID, EMB), HID)}
    _L3_ffn_all = _L3_ffn_setup()
    _L3_ffn_in = {k: v for k, v in _L3_ffn_all.items() if k in ('ln1_scale', 'ln1_shift', 'wq', 'wk', 'wv', 'wo', 'bo', 'ln2_scale', 'ln2_shift', 'gate_w', 'w1', 'w2', 'w3')}
    del _L3_ffn_all
    return {'x': x, 'ctx_1024': ctx_1024, 'mask_BxSxS2_ik1': mask_BxSxS2_ik1, 'mask_Bx1xSxS2_bk1': mask_Bx1xSxS2_bk1, 'g_xattn': g_xattn, 'g_ffn': g_ffn, 'L0_xattn_Wq': _L0_xattn_in['Wq'], 'L0_xattn_Wk': _L0_xattn_in['Wk'], 'L0_xattn_Wv': _L0_xattn_in['Wv'], 'L0_xattn_Wo': _L0_xattn_in['Wo'], 'L0_ffn_Wp': _L0_ffn_in['Wp'], 'L0_ffn_sim_matrix': _L0_ffn_in['sim_matrix'], 'L0_ffn_temperature': _L0_ffn_in['temperature'], 'L0_ffn_W1': _L0_ffn_in['W1'], 'L0_ffn_b1': _L0_ffn_in['b1'], 'L0_ffn_W2': _L0_ffn_in['W2'], 'L0_ffn_b2': _L0_ffn_in['b2'], 'L1_xattn_w_q': _L1_xattn_in['w_q'], 'L1_xattn_w_k': _L1_xattn_in['w_k'], 'L1_xattn_w_v': _L1_xattn_in['w_v'], 'L1_xattn_w_o': _L1_xattn_in['w_o'], 'L1_ffn_fast_b': _L1_ffn_in['fast_b'], 'L1_ffn_w_fc': _L1_ffn_in['w_fc'], 'L1_ffn_w_proj': _L1_ffn_in['w_proj'], 'L1_ffn_u': _L1_ffn_in['u'], 'L1_ffn_v': _L1_ffn_in['v'], 'L1_ffn_gate': _L1_ffn_in['gate'], 'L2_xattn_wq_w': _L2_xattn_in['wq_w'], 'L2_xattn_wq_b': _L2_xattn_in['wq_b'], 'L2_xattn_wk_w': _L2_xattn_in['wk_w'], 'L2_xattn_wk_b': _L2_xattn_in['wk_b'], 'L2_xattn_wv_w': _L2_xattn_in['wv_w'], 'L2_xattn_wv_b': _L2_xattn_in['wv_b'], 'L2_xattn_mk': _L2_xattn_in['mk'], 'L2_xattn_mv': _L2_xattn_in['mv'], 'L2_xattn_wo_w': _L2_xattn_in['wo_w'], 'L2_xattn_wo_b': _L2_xattn_in['wo_b'], 'L2_ffn_gate_w': _L2_ffn_in['gate_w'], 'L2_ffn_w1': _L2_ffn_in['w1'], 'L2_ffn_b1': _L2_ffn_in['b1'], 'L2_ffn_w2': _L2_ffn_in['w2'], 'L2_ffn_b2': _L2_ffn_in['b2'], 'L3_xattn_Wq': _L3_xattn_in['Wq'], 'L3_xattn_bq': _L3_xattn_in['bq'], 'L3_xattn_Wk': _L3_xattn_in['Wk'], 'L3_xattn_bk': _L3_xattn_in['bk'], 'L3_xattn_Wv': _L3_xattn_in['Wv'], 'L3_xattn_bv': _L3_xattn_in['bv'], 'L3_xattn_Wo': _L3_xattn_in['Wo'], 'L3_xattn_bo': _L3_xattn_in['bo'], 'L3_ffn_ln1_scale': _L3_ffn_in['ln1_scale'], 'L3_ffn_ln1_shift': _L3_ffn_in['ln1_shift'], 'L3_ffn_wq': _L3_ffn_in['wq'], 'L3_ffn_wk': _L3_ffn_in['wk'], 'L3_ffn_wv': _L3_ffn_in['wv'], 'L3_ffn_wo': _L3_ffn_in['wo'], 'L3_ffn_bo': _L3_ffn_in['bo'], 'L3_ffn_ln2_scale': _L3_ffn_in['ln2_scale'], 'L3_ffn_ln2_shift': _L3_ffn_in['ln2_shift'], 'L3_ffn_gate_w': _L3_ffn_in['gate_w'], 'L3_ffn_w1': _L3_ffn_in['w1'], 'L3_ffn_w2': _L3_ffn_in['w2'], 'L3_ffn_w3': _L3_ffn_in['w3']}

def reference(x, ctx_1024, mask_BxSxS2_ik1, mask_Bx1xSxS2_bk1, g_xattn, g_ffn, L0_xattn_Wq, L0_xattn_Wk, L0_xattn_Wv, L0_xattn_Wo, L0_ffn_Wp, L0_ffn_sim_matrix, L0_ffn_temperature, L0_ffn_W1, L0_ffn_b1, L0_ffn_W2, L0_ffn_b2, L1_xattn_w_q, L1_xattn_w_k, L1_xattn_w_v, L1_xattn_w_o, L1_ffn_fast_b, L1_ffn_w_fc, L1_ffn_w_proj, L1_ffn_u, L1_ffn_v, L1_ffn_gate, L2_xattn_wq_w, L2_xattn_wq_b, L2_xattn_wk_w, L2_xattn_wk_b, L2_xattn_wv_w, L2_xattn_wv_b, L2_xattn_mk, L2_xattn_mv, L2_xattn_wo_w, L2_xattn_wo_b, L2_ffn_gate_w, L2_ffn_w1, L2_ffn_b1, L2_ffn_w2, L2_ffn_b2, L3_xattn_Wq, L3_xattn_bq, L3_xattn_Wk, L3_xattn_bk, L3_xattn_Wv, L3_xattn_bv, L3_xattn_Wo, L3_xattn_bo, L3_ffn_ln1_scale, L3_ffn_ln1_shift, L3_ffn_wq, L3_ffn_wk, L3_ffn_wv, L3_ffn_wo, L3_ffn_bo, L3_ffn_ln2_scale, L3_ffn_ln2_shift, L3_ffn_gate_w, L3_ffn_w1, L3_ffn_w2, L3_ffn_w3):
    import jax
    import jax.numpy as jnp

    def _L0_xattn_ref(inputs, embbeding_V, embbeding_K, Wq, Wk, Wv, Wo):
        import jax, jax.numpy as jnp
        import numpy as np
        B, S, E, H = (2, 256, 128, 16)
        D = E // H
        b = inputs.shape[0]
        x = jnp.broadcast_to(inputs[:, -1, :][:, None, :], (b, S, E))
        q = (x @ Wq.T).reshape(b, S, H, D).transpose(0, 2, 1, 3)
        k = (embbeding_K @ Wk.T).reshape(b, S, H, D).transpose(0, 2, 1, 3)
        v = (embbeding_V @ Wv.T).reshape(b, S, H, D).transpose(0, 2, 1, 3)
        s = jnp.einsum('bhqd,bhkd->bhqk', q, k)
        p = jax.nn.softmax(s, axis=-1)
        o = jnp.einsum('bhqk,bhkd->bhqd', p, v)
        o = o.transpose(0, 2, 1, 3).reshape(b, S, E)
        return o @ Wo.T

    def _L0_ffn_ref(x, Wp, sim_matrix, temperature, W1, b1, W2, b2):
        import jax, jax.numpy as jnp
        import numpy as np
        EPS = 1e-12

        def _l2norm(v):
            n = jnp.sqrt(jnp.sum(v * v, axis=-1, keepdims=True))
            return v / jnp.maximum(n, EPS)
        E = sim_matrix.shape[0]
        top_k = 2
        proj = jnp.einsum('bsd,ed->bse', x, Wp)
        pn = _l2norm(proj)
        sn = _l2norm(sim_matrix)
        gate_scores = jnp.einsum('bsd,ed->bse', pn, sn) / temperature
        top_v, top_i = jax.lax.top_k(gate_scores, top_k)
        gate_probs = jax.nn.softmax(top_v, axis=-1)
        comb = jnp.sum(jax.nn.one_hot(top_i, E, dtype=x.dtype) * gate_probs[..., None], axis=-2)
        h = jax.nn.gelu(jnp.einsum('bsd,edf->ebsf', x, W1) + b1[:, None, None, :], approximate=False)
        eo = jnp.einsum('ebsf,efd->ebsd', h, W2) + b2[:, None, None, :]
        out = jnp.einsum('ebsd,bse->bsd', eo, comb)
        return out

    def _L1_xattn_ref(query, key, value, mask, w_q, w_k, w_v, w_o):
        import jax, jax.numpy as jnp
        import numpy as np
        B, S, D, H = (2, 256, 128, 16)
        DK = D // H
        b, s, d = query.shape
        Q = jnp.einsum('bsd,ed->bse', query, w_q).reshape(b, s, H, DK).transpose(0, 2, 1, 3)
        K = jnp.einsum('bsd,ed->bse', key, w_k).reshape(b, s, H, DK).transpose(0, 2, 1, 3)
        V = jnp.einsum('bsd,ed->bse', value, w_v).reshape(b, s, H, DK).transpose(0, 2, 1, 3)
        scale = jnp.float32(DK ** 0.5)
        scores = jnp.einsum('bhqd,bhkd->bhqk', Q, K) / scale
        scores = jnp.where(mask[:, None, :, :] == 0, jnp.float32(-1000000000.0), scores)
        attn = jax.nn.softmax(scores, axis=-1)
        out = jnp.einsum('bhqk,bhkd->bhqd', attn, V)
        out = out.transpose(0, 2, 1, 3).reshape(b, s, d)
        return jnp.einsum('bsd,ed->bse', out, w_o)

    def _L1_ffn_ref(x, fast_b, w_fc, w_proj, u, v, gate):
        import jax, jax.numpy as jnp
        import numpy as np

        def _bitlinear(x, w_latent):
            scale = jax.lax.stop_gradient(jnp.clip(jnp.mean(jnp.abs(w_latent), axis=1, keepdims=True), 1e-05, None))
            tern = jnp.clip(jnp.round(w_latent / scale), -1.0, 1.0)
            w = w_latent + jax.lax.stop_gradient(tern - w_latent)
            return x @ (w * scale).T
        h = _bitlinear(x, w_fc) + gate * (x @ v.T @ fast_b.T @ u.T)
        r = jnp.maximum(h, 0.0)
        return _bitlinear(r * r, w_proj)

    def _L2_xattn_ref(queries, keys, values, wq_w, wq_b, wk_w, wk_b, wv_w, wv_b, mk, mv, wo_w, wo_b):
        import jax, jax.numpy as jnp
        import numpy as np
        H, DK, DV = (16, 64, 64)
        MEM = 128
        D_MODEL = 128
        OUT_DIM = 128
        B, S, _ = queries.shape
        q = (queries @ wq_w + wq_b).reshape(B, S, H, DK).transpose(0, 2, 1, 3)
        k_proj = keys @ wk_w + wk_b
        v_proj = values @ wv_w + wv_b
        k_ext = jnp.concatenate([k_proj, jnp.broadcast_to(mk, (B, MEM, H * DK))], axis=1)
        v_ext = jnp.concatenate([v_proj, jnp.broadcast_to(mv, (B, MEM, H * DV))], axis=1)
        T = S + MEM
        k = k_ext.reshape(B, T, H, DK).transpose(0, 2, 1, 3)
        v = v_ext.reshape(B, T, H, DV).transpose(0, 2, 1, 3)
        scores = jnp.einsum('bhsd,bhtd->bhst', q, k) / jnp.sqrt(jnp.float32(DK))
        attn = jax.nn.softmax(scores, axis=-1)
        out = jnp.einsum('bhst,bhtd->bhsd', attn, v)
        out = out.transpose(0, 2, 1, 3).reshape(B, S, H * DV)
        return out @ wo_w + wo_b

    def _L2_ffn_ref(x, gate_w, w1, b1, w2, b2):
        import jax, jax.numpy as jnp
        import numpy as np
        TEMPERATURE = 1.0
        TOPK = 2
        s, b, h = x.shape
        x_flat = x.reshape(s * b, h)
        logits = x_flat @ gate_w.T
        probs = jax.nn.softmax(logits / TEMPERATURE, axis=-1)
        topk_probs, topk_idx = jax.lax.top_k(probs, TOPK)
        hidden = jax.nn.relu(jnp.einsum('th,ehf->tef', x_flat, w1) + b1[None])
        all_out = jnp.einsum('tef,efh->teh', hidden, w2) + b2[None]
        gathered = jnp.take_along_axis(all_out, topk_idx[:, :, None], axis=1)
        y_flat = jnp.sum(gathered * topk_probs[:, :, None], axis=1)
        return y_flat.reshape(s, b, h)

    def _L3_xattn_ref(queries, keys, values, mask, Wq, bq, Wk, bk, Wv, bv, Wo, bo):
        import jax, jax.numpy as jnp
        import numpy as np
        B, S, D, H = (4, 256, 128, 16)
        HD = D // H
        b, sq, d = queries.shape

        def split_heads(x):
            return x.reshape(b, x.shape[1], H, HD).transpose(0, 2, 1, 3)
        q = split_heads(queries @ Wq + bq)
        k = split_heads(keys @ Wk + bk)
        v = split_heads(values @ Wv + bv)
        scores = jnp.einsum('bhqd,bhkd->bhqk', q, k) / jnp.sqrt(jnp.float32(HD))
        scores = jnp.where(mask, jnp.float32(-1000000000000000.0), scores)
        attn = jax.nn.softmax(scores, axis=-1)
        ctx = jnp.einsum('bhqk,bhkd->bhqd', attn, v)
        ctx = ctx.transpose(0, 2, 1, 3).reshape(b, sq, d)
        return ctx @ Wo + bo

    def _L3_ffn_ref(x, ln1_scale, ln1_shift, wq, wk, wv, wo, bo, ln2_scale, ln2_shift, gate_w, w1, w2, w3):
        import jax, jax.numpy as jnp
        import numpy as np
        EMB = 128
        HID = 256
        HEADS = 16
        HEAD_DIM = EMB // HEADS
        EXPERTS = 8
        TOPK = 2
        EPS = 1e-05

        def layernorm(x, scale, shift):
            mean = jnp.mean(x, axis=-1, keepdims=True)
            var = jnp.mean((x - mean) ** 2, axis=-1, keepdims=True)
            return scale * (x - mean) / jnp.sqrt(var + EPS) + shift

        def attention(x, wq, wk, wv, wo, bo):
            b, t, _ = x.shape
            q = (x @ wq).reshape(b, t, HEADS, HEAD_DIM)
            k = (x @ wk).reshape(b, t, HEADS, HEAD_DIM)
            v = (x @ wv).reshape(b, t, HEADS, HEAD_DIM)
            scores = jnp.einsum('bqhd,bkhd->bhqk', q, k)
            mask = jnp.arange(t)[:, None] < jnp.arange(t)[None, :]
            scores = jnp.where(mask, -jnp.inf, scores)
            attn = jax.nn.softmax(scores / np.sqrt(HEAD_DIM), axis=-1)
            ctx = jnp.einsum('bhqk,bkhd->bqhd', attn, v).reshape(b, t, EMB)
            return ctx @ wo + bo

        def moe_ff(x, gate_w, w1, w2, w3):
            b, t, d = x.shape
            xf = x.reshape(b * t, d)
            scores = xf @ gate_w
            topk_scores, topk_idx = jax.lax.top_k(scores, TOPK)
            topk_probs = jax.nn.softmax(topk_scores, axis=-1)
            weight = jnp.sum(jax.nn.one_hot(topk_idx, EXPERTS, dtype=xf.dtype) * topk_probs[..., None], axis=1)
            h = jax.nn.silu(jnp.einsum('td,edh->eth', xf, w1)) * jnp.einsum('td,edh->eth', xf, w2)
            out_e = jnp.einsum('eth,ehd->etd', h, w3)
            out = jnp.einsum('etd,te->td', out_e, weight)
            return out.reshape(b, t, d)
        h = layernorm(x, ln1_scale, ln1_shift)
        x = x + attention(h, wq, wk, wv, wo, bo)
        h = layernorm(x, ln2_scale, ln2_shift)
        x = x + moe_ff(h, gate_w, w1, w2, w3)
        return x
    x = x + jnp.tanh(g_xattn[0]) * _L0_xattn_ref(_layernorm(x, axis=-1), ctx_1024, ctx_1024, L0_xattn_Wq, L0_xattn_Wk, L0_xattn_Wv, L0_xattn_Wo)
    x = x + jnp.tanh(g_ffn[0]) * _L0_ffn_ref(_layernorm(x, axis=-1), L0_ffn_Wp, L0_ffn_sim_matrix, L0_ffn_temperature, L0_ffn_W1, L0_ffn_b1, L0_ffn_W2, L0_ffn_b2)
    x = x + jnp.tanh(g_xattn[1]) * _L1_xattn_ref(_layernorm(x, axis=-1), ctx_1024, ctx_1024, mask_BxSxS2_ik1, L1_xattn_w_q, L1_xattn_w_k, L1_xattn_w_v, L1_xattn_w_o)
    x = x + jnp.tanh(g_ffn[1]) * _L1_ffn_ref(_layernorm(x, axis=-1), L1_ffn_fast_b, L1_ffn_w_fc, L1_ffn_w_proj, L1_ffn_u, L1_ffn_v, L1_ffn_gate)
    x = x + jnp.tanh(g_xattn[2]) * _L2_xattn_ref(_layernorm(x, axis=-1), ctx_1024, ctx_1024, L2_xattn_wq_w, L2_xattn_wq_b, L2_xattn_wk_w, L2_xattn_wk_b, L2_xattn_wv_w, L2_xattn_wv_b, L2_xattn_mk, L2_xattn_mv, L2_xattn_wo_w, L2_xattn_wo_b)
    x = x + jnp.tanh(g_ffn[2]) * _L2_ffn_ref(_layernorm(x, axis=-1), L2_ffn_gate_w, L2_ffn_w1, L2_ffn_b1, L2_ffn_w2, L2_ffn_b2)
    x = x + jnp.tanh(g_xattn[3]) * _L3_xattn_ref(_layernorm(x, axis=-1), ctx_1024, ctx_1024, mask_Bx1xSxS2_bk1, L3_xattn_Wq, L3_xattn_bq, L3_xattn_Wk, L3_xattn_bk, L3_xattn_Wv, L3_xattn_bv, L3_xattn_Wo, L3_xattn_bo)
    x = x + jnp.tanh(g_ffn[3]) * _L3_ffn_ref(_layernorm(x, axis=-1), L3_ffn_ln1_scale, L3_ffn_ln1_shift, L3_ffn_wq, L3_ffn_wk, L3_ffn_wv, L3_ffn_wo, L3_ffn_bo, L3_ffn_ln2_scale, L3_ffn_ln2_shift, L3_ffn_gate_w, L3_ffn_w1, L3_ffn_w2, L3_ffn_w3)
    return x

_drawn_inputs = setup_inputs


def setup_inputs(seed=0):
    import zlib

    import numpy as np

    out = dict(_drawn_inputs(seed))
    spreads = {'L0_ffn_b1': (0.0, 0.1),
     'L0_ffn_b2': (0.0, 0.1),
     'L2_xattn_wq_b': (0.0, 1.721),
     'L2_xattn_wk_b': (0.0, 2.0),
     'L2_xattn_wv_b': (0.0, 0.468),
     'L2_xattn_wo_b': (0.0, 0.336),
     'L2_ffn_b1': (0.0, 1.067),
     'L2_ffn_b2': (0.0, 0.595),
     'L3_xattn_bq': (0.0, 1.273),
     'L3_xattn_bk': (0.0, 2.0),
     'L3_xattn_bv': (0.0, 0.388),
     'L3_xattn_bo': (0.0, 0.41),
     'L3_ffn_ln1_scale': (1.0, 0.2),
     'L3_ffn_ln1_shift': (0.0, 0.1),
     'L3_ffn_bo': (0.0, 0.27),
     'L3_ffn_ln2_scale': (1.0, 0.2),
     'L3_ffn_ln2_shift': (0.0, 0.419)}
    factors = {'g_ffn': 22.128,
     'L0_xattn_Wq': 4.908,
     'L0_xattn_Wk': 4.265,
     'L1_ffn_fast_b': 8.0,
     'L1_ffn_w_fc': 3.362,
     'L1_ffn_w_proj': 2.947,
     'L1_ffn_u': 8.0,
     'L1_ffn_v': 8.0,
     'L2_xattn_mk': 64.0,
     'L2_xattn_mv': 64.0}
    for name, (base, spread) in spreads.items():
        noise = np.random.default_rng([zlib.crc32(name.encode()), seed]).standard_normal(out[name].shape)
        drawn = base * np.exp(spread * noise) if base else spread * noise
        out[name] = jnp.asarray(drawn.astype(out[name].dtype))
    for name, factor in factors.items():
        out[name] = (out[name] * factor).astype(out[name].dtype)
    return out
```

```python
from contextlib import ExitStack, contextmanager

import numpy as np

import concourse.bass as bass
from concourse import mybir

F32 = mybir.dt.float32
F32R = mybir.dt.float32r
BF16 = mybir.dt.bfloat16
I32 = mybir.dt.int32
U32 = mybir.dt.uint32
U8 = mybir.dt.uint8
ACT = mybir.ActivationFunctionType
ALU = mybir.AluOpType
AX = mybir.AxisListType

P = 128
B, S, D = 8, 256, 128
H = 16
HD = D // H
TPB = S // P
NT = B * TPB
E = 8
CH = 4
NC = NT // CH
CW = CH * P
LN_EPS = 1e-5
MASKED = -2.0 ** 100
Q32 = 32
GH = 4
NG = H // GH
DK2 = 64
MEM = 128
NK2 = (S + MEM) // P


class Signal:

    def __init__(self, sem):
        self.sem, self.given = sem, 0


class Count:

    def __init__(self, signal, total):
        self.sem, self.start = signal.sem, signal.given
        signal.given += total

    def __call__(self, n):
        return self.sem, self.start + n


class Order:

    def __init__(self, eng, sem):
        self.eng, self.sem, self.given, self.turned = eng, sem, 0, 0

    def mark(self, instruction):
        instruction.then_inc(self.sem, 1)
        self.given += 1

    def wait(self):
        self.eng.wait_ge(self.sem, self.turned + self.given)

    @contextmanager
    def turns(self, i, n, each):
        start = self.given
        self.turned = i * each
        yield
        assert self.given - start == each, f"{self.given - start} marks a turn"
        self.given, self.turned = start + n * each, 0


def spread(ap, axis, n):
    shape = list(ap.shape)
    shape.insert(axis, n)
    return ap.unsqueeze(axis).to_broadcast(shape)

C_MHALF = 0
C_HALF = C_MHALF + CH
C_E = C_HALF + CH + 0
C_IOTA = C_E + CH * (E + 1)
C_HEADS = C_IOTA + E
C_SPLIT = C_HEADS + Q32
C_ONES = C_SPLIT + 3
C_TEMP = C_ONES + 1
C_L1GATE = C_TEMP + 1
C_RAWGATES = C_L1GATE + 1
N_CONSTS = C_RAWGATES + 8
S_B2 = E * 4
S_PROJ = S_B2 + D
S_GATE = S_PROJ + D
S_AFFINE = S_GATE + E
N_SMALL = S_AFFINE + 2
CREDIT = {"up_drained": 4, "down_drained": 2, "down_full": 2, "mixed_full": 1, "mixed_drained": 1, "probs_drained": 1,
          "hidden_done": 1}


def apart(eng, core):
    eng.sem_inc(core.apart, 1)


class Core:

    def __init__(self, nc, ctx, ins):
        self.nc, self.ins = nc, ins

        def sb(name, shape, dt=F32):
            return ctx.enter_context(nc.sbuf_tensor(name, shape, dt))

        def psum(name, shape):
            return ctx.enter_context(nc.psum_tensor(name, shape, F32))

        self.scores = psum("scores", [P, 4, 512])
        self.probs_ps = psum("probs_ps", [P, 2, 512])
        self.mixed = psum("mixed", [P, 512])
        self.misc = psum("misc", [P, 512])

        self.x = sb("x", [P, NT, D])
        self.y = sb("y", [P, NT, D])
        self.consts = sb("consts", [P, N_CONSTS])
        self.ident = sb("ident", [P, P])
        self.ident_bf = sb("ident_bf", [P, P], BF16)
        self.gates = sb("gates", [P, 2, 4])
        self.ln_stats = sb("ln_stats", [P, CH, 6])
        self.ln_mv = sb("ln_mv", [P, CH, 2])
        self.ln_var = sb("ln_var", [P, CH])
        self.ln_rstd = sb("ln_rstd", [P, CH])
        self.xn = sb("xn", [P, CH, D])
        self.xnt = sb("xnt", [P, NT * P])
        self.xnt_stage = sb("xnt_stage", [P, CW])
        self.minus_half = self.consts[:, C_MHALF:C_MHALF + CH]
        self.w_up = sb("w_up", [P, E, 512])
        self.w_down = sb("w_down", [P, E, 4, D])
        self.shared = sb("shared", [P, 2, 2048])
        self.l1_up = sb("l1_up", [P, 512])
        self.l1_down = sb("l1_down", [P, 4, D])
        self.small = {n: sb(n + "small", [P, N_SMALL]) for n in ("l0_", "l2_", "l3_")}
        self.masks_causal = sb("masks_causal", [P, 2, TPB, S], BF16)
        self.inv_temperature = sb("inv_temperature", [P, 1])[:]
        self.comb = sb("comb", [P, NT, E])
        self.route = {n: sb("route_" + n, shape)[:] for n, shape in dict(
            norm=[P, CH], z=[P, CH], rz=[P, CH], ss=[P, CH], g=[P, CH, E], best=[P, CH, 8], d=[P, CH, E + 1],
            ex=[P, CH, E + 1], placef=[P, CH, 2], part=[P, 2, CH, E], p=[P, 2, CH], comb=[P, CH, E],
            comb_t=[E, CW], squares=[P, CH, P]).items()}
        self.route["is"] = sb("route_is", [P, 2, CH, E])[:]
        self.route["place"] = sb("route_place", [P, CH, 8], U32)[:]

        self.signals = {}
        self.ctx = ctx
        self.experts_used = self.attention_done = None
        (self.loaded_consts, self.loaded_setup, self.loaded_row, self.loaded_ctx, self.loaded_x, self.loaded_small,
         self.loaded_stored, self.loaded_causal) = (ctx.enter_context(nc.semaphore("loaded_" + name)) for name in (
             "consts", "setup", "row", "ctx", "x", "small", "stored", "causal"))
        self.small_ready = (self.loaded_small, 16 * len(self.small))
        self.apart = ctx.enter_context(nc.semaphore("apart"))
        for name, n in CREDIT.items():
            self.count(name, n)

    def count(self, name, total):
        if name not in self.signals:
            self.signals[name] = Signal(self.ctx.enter_context(self.nc.semaphore(name)))
        return Count(self.signals[name], total)


    def ln_vector_stats(self, dve, order, src, n, done, nth):
        nc = self.nc
        rows = src.shape[0]
        order.wait()
        for t in range(n):
            ins = nc.vector.bn_stats(self.ln_stats[0:rows, t, :], src[:, t, :])
            if t == n - 1:
                order.mark(ins)
        order.wait()
        apart(dve, self)
        for t in range(n):
            ins = nc.vector.bn_aggr(self.ln_mv[0:rows, t, :], self.ln_stats[0:rows, t, :])
        ins.then_inc(done.sem, 1)

    def ln_pool(self, pool, order, n, stats, rstd, nth, rows=P):
        nc = self.nc
        pool.wait_ge(*stats(nth))
        apart(pool, self)
        order.mark(nc.gpsimd.tensor_scalar(self.ln_var[0:rows, 0:n], self.ln_mv[0:rows, 0:n, 1],
                                           LN_EPS, None, ALU.add))
        order.wait()
        nc.gpsimd.tensor_tensor(self.ln_rstd[0:rows, 0:n], self.ln_var[0:rows, 0:n],
                                self.minus_half[0:rows, 0:n], ALU.pow).then_inc(rstd.sem, 1)

    def ln_vector_scale(self, dve, src, n, rstd, done, nth, out=None):
        nc = self.nc
        rows = src.shape[0]
        dve.wait_ge(*rstd(nth))
        for t in range(n):
            ins = nc.vector.tensor_scalar((self.xn if out is None else out)[0:rows, t, :], src[:, t, :],
                                          self.ln_mv[0:rows, t, 0:1], self.ln_rstd[0:rows, t:t + 1],
                                          ALU.subtract, ALU.mult)
        ins.then_inc(done.sem, 1)


class Setup:

    def __init__(self, core):
        self.k = core
        c = core.count
        self.misc_full, self.misc_drained = c("misc_full", 6), c("misc_drained", 6)
        core.gates_done = c("gates_done", 1)
        self.norm = c("route_norm", 1)
        self.squared, self.unit, self.ternary = c("sim_squared", 1), c("sim_unit", 1), c("ternary_done", 2)
        nc = core.nc

        def sb(name, shape):
            return core.ctx.enter_context(nc.sbuf_tensor(name, shape, F32))

        self.sim = sb("sim", [E, 3, D])
        self.sim_n = sb("sim_n", [E, 4])
        self.unit_t = sb("sim_unit_t", [P, E])
        self.wp = sb("wp", [P, D])
        self.lora = sb("lora", [16, 16 + D + 512])
        self.lora_m = sb("lora_m", [16, D])
        self.scale = sb("tern_scale", [P, 2, 3, 4])
        self.w = core.shared[:, 0, 0:1024].rearrange("p (j n) -> p j n", j=2)
        self.a = core.shared[:, 0, 1024:2048].rearrange("p (j n) -> p j n", j=2)
        self.b = core.shared[:, 1, 0:1024].rearrange("p (j n) -> p j n", j=2)
        self.fct = core.shared[:, 1, 1024:1536]

    def tensor(self, pe):
        k, nc = self.k, self.k.nc
        misc = k.misc
        pe.wait_ge(k.loaded_consts, 32)
        pe.wait_ge(*self.unit(1))
        nc.tensor.transpose(misc[:, 0:E], self.sim[:, 2, :], k.ident[0:E, 0:E]).then_inc(self.misc_full.sem, 1)
        pe.wait_ge(k.loaded_setup, 64)
        pe.wait_ge(*self.misc_drained(1))
        nc.tensor.matmul(misc[:, 0:E], self.wp[:], self.unit_t[:], start=True, stop=True)\
            .then_inc(self.misc_full.sem, 1)
        pe.wait_ge(*self.misc_drained(2))
        pe.wait_ge(*self.ternary(1))
        for t in range(4):
            ins = nc.tensor.transpose(misc[:, t * P:(t + 1) * P], self.b[:, 0, t * P:(t + 1) * P], k.ident[:])
        ins.then_inc(self.misc_full.sem, 1)
        pe.wait_ge(*self.misc_drained(3))
        nc.tensor.matmul(misc[0:16, 0:D], self.lora[:, 0:16], self.lora[:, 16:16 + D], start=True, stop=True)\
            .then_inc(self.misc_full.sem, 1)
        pe.wait_ge(*self.misc_drained(4))
        nc.tensor.matmul(misc[:], self.lora_m[:], self.lora[:, 16 + D:], start=True, stop=True)\
            .then_inc(self.misc_full.sem, 1)
        pe.wait_ge(*self.misc_drained(5))
        pe.wait_ge(*self.ternary(2))
        for t in range(4):
            ins = nc.tensor.transpose(misc[:, t * P:(t + 1) * P], self.b[:, 1, t * P:(t + 1) * P], k.ident[:])
        ins.then_inc(self.misc_full.sem, 1)

    def ternary_weights(self, dve, order, j):
        nc = self.k.nc
        rows = 4 if j == 0 else 1
        w, a, b = (v[:, j, :].rearrange("p (t n) -> p t n", t=rows) for v in (self.w, self.a, self.b))
        s, up, low = (self.scale[:, j, i, 0:rows] for i in range(3))

        def step(ins):
            order.mark(ins)
            order.wait()

        n = 512 // rows

        def row(v):
            return spread(v, 2, n)

        step(nc.vector.tensor_reduce(s, w, AX.X, ALU.add, apply_absolute_value=True))
        step(nc.vector.tensor_scalar(s, s, 1.0 / n, 1e-5, ALU.mult, ALU.max))
        order.mark(nc.vector.tensor_scalar(up, s, 0.5, None, ALU.mult))
        step(nc.vector.tensor_scalar(low, s, -0.5, None, ALU.mult))
        order.mark(nc.vector.tensor_tensor(a, w, row(up), ALU.is_gt))
        step(nc.vector.tensor_tensor(b, w, row(low), ALU.is_lt))
        step(nc.vector.tensor_tensor(a, a, b, ALU.subtract))
        step(nc.vector.tensor_tensor(a, a, w, ALU.subtract))
        step(nc.vector.tensor_tensor(a, a, w, ALU.add))
        nc.vector.tensor_tensor(b, a, row(s), ALU.mult).then_inc(self.ternary.sem, 1)

    def vector(self, dve, order):
        k, nc = self.k, self.k.nc
        misc = k.misc
        dve.wait_ge(k.loaded_setup, 64)
        order.mark(nc.vector.tensor_tensor(self.sim[:, 1, :], self.sim[:, 0, :], self.sim[:, 0, :], ALU.mult))
        order.wait()
        nc.vector.tensor_reduce(self.sim_n[:, 0:1], self.sim[:, 1, :], AX.X, ALU.add).then_inc(self.squared.sem, 1)
        dve.wait_ge(k.loaded_consts, 32)
        order.mark(nc.vector.reciprocal(k.inv_temperature, k.consts[:, C_TEMP:C_TEMP + 1]))
        self.ternary_weights(dve, order, 0)
        dve.wait_ge(*self.norm(1))
        order.mark(nc.vector.tensor_scalar(self.sim_n[:, 2:3], self.sim_n[:, 1:2], 1e-12, None, ALU.max))
        order.wait()
        order.mark(nc.vector.reciprocal(self.sim_n[:, 3:4], self.sim_n[:, 2:3]))
        order.wait()
        nc.vector.tensor_scalar(self.sim[:, 2, :], self.sim[:, 0, :], self.sim_n[:, 3:4], None, ALU.mult)\
            .then_inc(self.unit.sem, 1)
        self.ternary_weights(dve, order, 1)
        dve.wait_ge(*self.misc_full(1))
        nc.vector.tensor_copy(self.unit_t[:], misc[:, 0:E]).then_inc(self.misc_drained.sem, 1)
        dve.wait_ge(*k.small_ready)
        dve.wait_ge(*self.misc_full(2))
        nc.vector.tensor_copy(k.small["l0_"][:, S_GATE:S_GATE + E], misc[:, 0:E]).then_inc(self.misc_drained.sem, 1)
        dve.wait_ge(*self.misc_full(3))
        nc.vector.tensor_copy(self.fct, misc[:]).then_inc(self.misc_drained.sem, 1)
        dve.wait_ge(*self.misc_full(4))
        nc.vector.tensor_copy(self.lora_m[:], misc[0:16, 0:D]).then_inc(self.misc_drained.sem, 1)
        dve.wait_ge(*self.misc_full(5))
        dve.wait_ge(*self.misc_drained(3))
        nc.vector.scalar_tensor_tensor(out=k.l1_up[:], in0=misc[:], scalar=k.consts[:, C_L1GATE:C_L1GATE + 1],
                                       in1=self.fct, op0=ALU.mult, op1=ALU.add).then_inc(self.misc_drained.sem, 1)
        dve.wait_ge(*self.misc_full(6))
        nc.vector.tensor_copy(k.l1_down[:], misc[:].rearrange("p (f d) -> p f d", f=4))\
            .then_inc(self.misc_drained.sem, 1)

    def scalar(self, act, order):
        k, nc = self.k, self.k.nc
        act.wait_ge(k.loaded_consts, 32)
        nc.scalar.activation(k.gates[:].rearrange("p a b -> p (a b)"), k.consts[:, C_RAWGATES:C_RAWGATES + 8],
                             ACT.Tanh).then_inc(k.gates_done.sem, 1)

    def gpsimd(self, pool, order):
        k, nc = self.k, self.k.nc
        pool.wait_ge(k.loaded_consts, 32)
        pool.wait_ge(*self.squared(1))
        nc.gpsimd.tensor_tensor(self.sim_n[:, 1:2], self.sim_n[:, 0:1], k.consts[0:E, C_HALF:C_HALF + 1], ALU.pow)\
            .then_inc(self.norm.sem, 1)

    def load_first(self, sp):
        k, ins = self.k, self.k.ins
        sp.dma_start(k.consts[:], ins["consts"]).then_inc(k.loaded_consts, 16)
        sp.dma_start(k.ident[:], ins["ident"]).then_inc(k.loaded_consts, 16)

    def sync(self, sp):
        k, ins = self.k, self.k.ins
        sp.dma_start(self.sim[:, 0, :], ins["l0_sim"]).then_inc(k.loaded_setup, 16)
        sp.dma_start(self.w, ins["l1_latent"]).then_inc(k.loaded_setup, 16)
        sp.dma_start(self.lora[:], ins["l1_lora"]).then_inc(k.loaded_setup, 16)
        sp.dma_start(self.wp[:], ins["l0_wp"]).then_inc(k.loaded_setup, 16)
        for name, t in k.small.items():
            sp.dma_start(t[:], ins[name + "small"]).then_inc(k.loaded_small, 16)
        sp.dma_start(k.x[:], ins["x"].rearrange("(n p) d -> p n d", p=P)).then_inc(k.loaded_x, 16)
        sp.dma_start(k.causal_raw, ins["causal"]).then_inc(k.loaded_causal, 16)


class RowAttention:

    def __init__(self, core, gate):
        self.k, self.gate = core, gate
        self.misc_full, self.misc_drained = core.count("misc_full", 6), core.count("misc_drained", 6)
        self.scores_full, self.scores_drained = core.count("scores_full", 2), core.count("scores_drained", 2)
        self.stats, self.rstd, self.normed = (core.count(f"ln_{n}", 1) for n in ("stats_done", "rstd_done", "normed"))
        self.max_done, self.probs_done, self.row_mixed = (core.count(f"row_{n}", 1) for n in ("max", "probs", "mixed"))
        self.x_written = self.scores_drained(2)
        nc = core.nc

        def sb(name, shape):
            return core.ctx.enter_context(nc.sbuf_tensor(name, shape, F32))

        self.x_last = sb("row_x_last", [B, 1, D])
        self.xl = sb("row_xl", [B, 1, D])
        self.xlt = sb("row_xlt", [P, B])
        self.w = sb("row_w", [P, 4, D])
        self.q_heads = sb("row_q_heads", [P, B, Q32])
        self.qk = sb("row_qk", [P, B * Q32])
        self.neg_max = sb("row_neg_max", [P, 2])
        self.sum = sb("row_sum", [P, 2])
        self.rsum = sb("row_rsum", [P, 2])
        self.mixed = sb("row_mixed_sb", [P, B])
        self.ctx_t = core.xnt
        self.ctx_n = core.y
        self.e = core.shared[:, 0, 0:512].rearrange("p (j s) -> p j s", j=2)
        self.p = core.shared[:, 0, 512:1024].rearrange("p (j s) -> p j s", j=2)
        self.pt = core.shared[:, 0, 1024:1536].rearrange("p (j t r) -> p j t r", j=2, t=2)
        self.ct = core.shared[:, 0, 1536:1792]
        self.picked = core.shared[:, 0, 1792:2048].rearrange("p (b h) -> p b h", b=B)

    def tensor(self, pe):
        k, nc = self.k, self.k.nc
        misc = k.misc
        pe.wait_ge(k.loaded_consts, 32)
        pe.wait_ge(*self.normed(1))
        nc.tensor.transpose(misc[:, 0:B], self.xl[:, 0, :], k.ident[0:B, 0:B]).then_inc(self.misc_full.sem, 1)
        pe.wait_ge(k.loaded_row, 32)
        pe.wait_ge(*self.misc_drained(1))
        nc.tensor.matmul(misc[:, 0:B], self.w[:, 0, :], self.xlt[:], start=True, stop=True)\
            .then_inc(self.misc_full.sem, 1)
        pe.wait_ge(*self.misc_drained(2))
        nc.tensor.matmul(misc[:, 0:B * Q32], self.w[:, 1, :], self.q_heads[:].rearrange("p b h -> p (b h)"),
                         start=True, stop=True).then_inc(self.misc_full.sem, 1)
        pe.wait_ge(*self.misc_drained(3))
        pe.wait_ge(k.loaded_ctx, 32)
        for b in range(B):
            r, j = Q32 * (b % 4), b // 4
            ins = nc.tensor.matmul(k.scores[r:r + Q32, 0, j * S:(j + 1) * S], self.qk[:, b * Q32:(b + 1) * Q32],
                                   self.ctx_t[:, b * S:(b + 1) * S], start=True, stop=True)
        ins.then_inc(self.scores_full.sem, 1)
        pe.wait_ge(*self.probs_done(1))
        for j in range(2):
            for t in range(TPB):
                n = (j * TPB + t) * P
                ins = nc.tensor.transpose(misc[:, n:n + P], self.p[:, j, t * P:(t + 1) * P], k.ident[:])
        ins.then_inc(self.misc_full.sem, 1)
        pe.wait_ge(*self.misc_drained(4))
        for b in range(B):
            for t in range(TPB):
                r = Q32 * (b % 4)
                ins = nc.tensor.matmul(misc[:, b * Q32:(b + 1) * Q32], self.ctx_n[:, TPB * b + t, :],
                                       self.pt[:, b // 4, t, r:r + Q32], start=(t == 0), stop=(t == TPB - 1))
        ins.then_inc(self.misc_full.sem, 1)
        pe.wait_ge(*self.misc_drained(5))
        nc.tensor.matmul(misc[:, 0:B * Q32], self.w[:, 2, :], self.ct, start=True, stop=True)\
            .then_inc(self.misc_full.sem, 1)
        pe.wait_ge(*self.row_mixed(1))
        pe.wait_ge(*self.scores_drained(1))
        out = k.scores[:, 0:2, :].rearrange("p a (b d) -> p (a b) d", d=D)
        for b in range(B):
            ins = nc.tensor.matmul(out[:, b, :], self.mixed[:, b:b + 1].to_broadcast([P, P]), self.w[:, 3, :],
                                   start=True, stop=True)
        ins.then_inc(self.scores_full.sem, 1)

    def vector(self, dve, order):
        k, nc = self.k, self.k.nc
        misc = k.misc
        dve.wait_ge(k.loaded_row, 32)
        k.ln_vector_stats(dve, order, self.x_last, 1, self.stats, 0)
        k.ln_vector_scale(dve, self.x_last, 1, self.rstd, self.normed, 1, out=self.xl)
        dve.wait_ge(*self.misc_full(1))
        nc.vector.tensor_copy(self.xlt[:], misc[:, 0:B]).then_inc(self.misc_drained.sem, 1)
        dve.wait_ge(*self.misc_full(2))
        head_of = k.consts[:, C_HEADS:C_HEADS + Q32]
        nc.vector.tensor_tensor(self.q_heads[:], spread(misc[:, 0:B], 2, Q32), spread(head_of, 1, B), ALU.mult)\
            .then_inc(self.misc_drained.sem, 1)
        dve.wait_ge(*self.misc_full(3))
        nc.vector.tensor_copy(self.qk[:], misc[:, 0:B * Q32]).then_inc(self.misc_drained.sem, 1)
        dve.wait_ge(*self.scores_full(1))
        nc.vector.tensor_reduce(self.neg_max[:], k.scores[:, 0, :].rearrange("p (j s) -> p j s", j=2), AX.X,
                                ALU.max, negate=True).then_inc(self.max_done.sem, 1)
        dve.wait_ge(*self.scores_drained(1))
        order.mark(nc.vector.reciprocal(self.rsum[:], self.sum[:]))
        order.wait()
        for j in range(2):
            ins = nc.vector.tensor_scalar(self.p[:, j, :], self.e[:, j, :], self.rsum[:, j:j + 1], None, ALU.mult)
        ins.then_inc(self.probs_done.sem, 1)
        dve.wait_ge(*self.misc_full(4))
        nc.vector.tensor_copy(self.pt, misc[:].rearrange("p (j t r) -> p j t r", j=2, t=2))\
            .then_inc(self.misc_drained.sem, 1)
        dve.wait_ge(*self.misc_full(5))
        nc.vector.tensor_copy(self.ct, misc[:, 0:B * Q32]).then_inc(self.misc_drained.sem, 1)
        dve.wait_ge(*self.misc_full(6))
        nc.vector.tensor_tensor(self.picked, misc[:, 0:B * Q32].rearrange("p (b h) -> p b h", b=B),
                                spread(head_of, 1, B), ALU.mult).then_inc(self.misc_drained.sem, 1)
        dve.wait_ge(*self.misc_drained(6))
        nc.vector.tensor_reduce(self.mixed[:], self.picked, AX.X, ALU.add).then_inc(self.row_mixed.sem, 1)
        dve.wait_ge(*self.scores_full(2))
        dve.wait_ge(k.loaded_x, 16)
        dve.wait_ge(*k.gates_done(1))
        out = k.scores[:, 0:2, :].rearrange("p a (b d) -> p (a b) d", d=D)
        for t in range(TPB):
            ins = nc.vector.scalar_tensor_tensor(out=k.x[:, t:NT:TPB, :], in0=out, scalar=self.gate,
                                                 in1=k.x[:, t:NT:TPB, :], op0=ALU.mult, op1=ALU.add)
        ins.then_inc(self.scores_drained.sem, 1)

    def gpsimd(self, pool, order):
        k = self.k
        pool.wait_ge(k.loaded_consts, 32)
        k.ln_pool(pool, order, 1, self.stats, self.rstd, 1, rows=B)

    def scalar(self, act, order):
        k, nc = self.k, self.k.nc
        act.wait_ge(*self.max_done(1))
        for j in range(2):
            ins = nc.scalar.activation(self.e[:, j, :], k.scores[:, 0, j * S:(j + 1) * S], ACT.Exp,
                                       bias=self.neg_max[:, j:j + 1], accum_out=self.sum[:, j:j + 1])
        ins.then_inc(self.scores_drained.sem, 1)

    def sync(self, sp):
        k, ins = self.k, self.k.ins
        sp.dma_start(self.x_last[:, 0, :], ins["x_last"]).then_inc(k.loaded_row, 16)
        sp.dma_start(self.w[:], ins["row_w"]).then_inc(k.loaded_row, 16)
        sp.dma_start(self.ctx_t[:], ins["ctx_t"]).then_inc(k.loaded_ctx, 16)
        sp.dma_start(self.ctx_n[:], ins["ctx_n"].rearrange("(n p) d -> p n d", p=P)).then_inc(k.loaded_ctx, 16)


class ExpertLayer:

    def __init__(self, core, kind, prefix, gate, before):
        self.k, self.kind, self.prefix, self.gate, self.before = core, kind, prefix, gate, before
        self.nf = 2 if kind == "gated" else 4
        self.m = {"cosine": 5, "softmax": 4, "gated": 2}[kind]
        self.src = core.y if kind == "gated" else core.x
        c = core.count
        self.misc_full, self.misc_drained = c("misc_full", NC * self.m), c("misc_drained", NC * self.m)
        self.up_full, self.up_drained = c("up_full", NC * E * 4), c("up_drained", NC * E * self.nf)
        self.hidden_done = c("hidden_done", NC * E * self.nf if kind == "gated" else 0)
        self.down_full, self.down_drained = c("down_full", NC * E), c("down_drained", NC * E)
        self.stats, self.rstd, self.normed = (c(f"ln_{n}", NC) for n in ("stats_done", "rstd_done", "normed"))
        self.xnt_ready, self.shifted, self.exps = c("xnt_ready", NC), c("route_shifted", NC), c("route_exp", NC)
        self.norms = c("route_norm", NC if kind == "cosine" else 0)
        self.comb_ready = c("comb_ready", NC)
        self.loaded = [c(f"loaded_experts{h}", 32) for h in range(2)]
        self.scores_drained, self.probs_drained, self.mixed_drained = (
            c(n, 0) for n in ("scores_drained", "probs_drained", "mixed_drained"))
        self.x_written = self.down_drained(NC * E)
        small = core.small[prefix]
        self.b1 = small[:, 0:E * 4].rearrange("p (e f) -> p e f", e=E)
        self.b2 = small[0:E, S_B2:S_B2 + D]
        self.w_proj = small[:, S_PROJ:S_PROJ + D]
        self.w_gate = small[:, S_GATE:S_GATE + E]
        self.affine = small[:, S_AFFINE:S_AFFINE + 2]
        self.r = core.route
        self.weights_free, core.experts_used = core.experts_used, self.down_full(NC * E)


    def tensor_transpose(self, pe, c):
        k, nc = self.k, self.k.nc
        pe.wait_ge(*self.misc_drained(self.m * c))
        pe.wait_ge(*self.normed(c + 1))
        for t in range(CH):
            ins = nc.tensor.transpose(k.misc[:, t * P:(t + 1) * P], k.xn[:, t, :], k.ident[:])
        ins.then_inc(self.misc_full.sem, 1)

    def tensor_route(self, pe, c):
        k, nc = self.k, self.k.nc
        n = self.m * c + 1
        if self.kind == "cosine":
            pe.wait_ge(*self.misc_drained(n))
            for t in range(CH):
                ins = nc.tensor.matmul(k.misc[:, t * P:(t + 1) * P], k.xnt_stage[:, t * P:(t + 1) * P], self.w_proj,
                                       start=True, stop=True)
            ins.then_inc(self.misc_full.sem, 1)
            n = n + 1
        pe.wait_ge(*self.misc_drained(n))
        for t in range(CH):
            ins = nc.tensor.matmul(k.misc[:, t * E:(t + 1) * E], k.xnt_stage[:, t * P:(t + 1) * P], self.w_gate,
                                   start=True, stop=True)
        ins.then_inc(self.misc_full.sem, 1)

    def tensor_comb(self, pe, c):
        k, nc = self.k, self.k.nc
        pe.wait_ge(*self.misc_drained(self.m * c + self.m - 2))
        pe.wait_ge(*self.comb_ready(c + 1))
        for t in range(CH):
            ins = nc.tensor.transpose(k.misc[0:E, t * P:(t + 1) * P], self.r["comb"][:, t, :], k.ident[:])
        ins.then_inc(self.misc_full.sem, 1)

    def tensor_bias(self, pe, c):
        k, nc = self.k, self.k.nc
        pe.wait_ge(*self.misc_drained(self.m * c + self.m - 1))
        for t in range(CH):
            ins = nc.tensor.matmul(k.misc[:, t * P:(t + 1) * P], self.r["comb_t"][0:E, t * P:(t + 1) * P], self.b2,
                                   start=True, stop=True)
        ins.then_inc(self.misc_full.sem, 1)

    def tensor_up(self, pe, c, e):
        k, nc = self.k, self.k.nc
        x = k.xnt[:, bass.ds(c * CW, CW)]
        n = (c * E + e) * 4
        d = (c * E + e) * self.nf
        for f in range(4):
            if self.kind != "gated":
                pe.wait_ge(*self.up_drained(n + f - 3))
            elif f < 2:
                pe.wait_ge(*self.up_drained(d + f - 1))
            else:
                pe.wait_ge(*self.hidden_done(d + f - 3))
            nc.tensor.matmul(k.scores[:, f, :], k.w_up[:, e, f * P:(f + 1) * P], x, start=True, stop=True)\
                .then_inc(self.up_full.sem, 1)

    def tensor_down(self, pe, c, e):
        k, nc = self.k, self.k.nc
        n = c * E + e
        pe.wait_ge(*self.down_drained(n - 1))
        done = self.hidden_done if self.kind == "gated" else self.up_drained
        pe.wait_ge(*done((n + 1) * self.nf))
        for t in range(CH):
            for f in range(self.nf):
                ins = nc.tensor.matmul(k.probs_ps[:, e % 2, t * P:(t + 1) * P],
                                       k.shared[:, e % 2, f * CW + t * P:f * CW + (t + 1) * P], k.w_down[:, e, f, :],
                                       start=(f == 0), stop=(f == self.nf - 1))
        ins.then_inc(self.down_full.sem, 1)

    def tensor_step(self, pe, c, prepare):
        pe.wait_ge(*self.xnt_ready(c + 1))
        biased = self.kind != "gated"
        for e in range(E + 1):
            if e < E:
                if e % 4 == 0:
                    pe.wait_ge(*self.loaded[e // 4](32))
                self.tensor_up(pe, c, e)
            if e:
                self.tensor_down(pe, c, e - 1)
            if prepare:
                if e == 3:
                    self.tensor_transpose(pe, c + 1)
                if e == 4:
                    self.tensor_route(pe, c + 1)
                if e == 6 and biased:
                    self.tensor_comb(pe, c + 1)
                if e == 7 and biased:
                    self.tensor_bias(pe, c + 1)

    def tensor(self, pe):
        for drained in (self.up_drained, self.down_drained, self.scores_drained,
                        self.probs_drained):
            pe.wait_ge(*drained(0))
        pe.wait_ge(*self.k.small_ready)
        self.tensor_transpose(pe, 0)
        self.tensor_route(pe, 0)
        if self.kind != "gated":
            self.tensor_comb(pe, 0)
            self.tensor_bias(pe, 0)
        with self.k.nc.tensor.Fori(0, NC - 1) as c:
            self.tensor_step(pe, c, True)
        self.tensor_step(pe, NC - 1, False)


    def vector_stats(self, dve, order, c):
        self.k.ln_vector_stats(dve, order, self.src[:, bass.ds(c * CH, CH), :], CH, self.stats, c)

    def vector_scale(self, dve, order, c):
        k, nc = self.k, self.k.nc
        dve.wait_ge(*self.misc_full(self.m * c))
        src = self.src[:, bass.ds(c * CH, CH), :]
        k.ln_vector_scale(dve, src, CH, self.rstd, self.normed, c + 1)
        if self.kind == "gated":
            x = k.x[:, bass.ds(c * CH, CH), :]
            order.mark(nc.vector.scalar_tensor_tensor(out=x, in0=src, scalar=self.gate, in1=x, op0=ALU.mult,
                                                      op1=ALU.add))

    def vector_xnt(self, dve, order, c):
        k, nc = self.k, self.k.nc
        dve.wait_ge(*self.misc_drained(self.m * c + 1))
        nc.vector.tensor_copy(k.xnt[:, bass.ds(c * CW, CW)], k.xnt_stage[:]).then_inc(self.xnt_ready.sem, 1)

    def vector_route(self, dve, order, c):
        k, nc, r = self.k, self.k.nc, self.r
        n = self.m * c + 1
        if self.kind == "cosine":
            n = n + 1
            dve.wait_ge(*self.norms(c + 1))
            order.mark(nc.vector.tensor_scalar(r["z"], r["norm"], 1e-12, None, ALU.max))
            order.wait()
            order.mark(nc.vector.reciprocal(r["rz"], r["z"]))
            order.wait()
            order.mark(nc.vector.tensor_scalar(r["rz"], r["rz"], k.inv_temperature, None, ALU.mult))
            order.wait()
        dve.wait_ge(*self.misc_full(n + 1))
        scores = k.misc[:, 0:CH * E].rearrange("p (t e) -> p t e", t=CH)
        if self.kind == "cosine":
            ins = nc.vector.tensor_tensor(r["g"], scores, spread(r["rz"], 2, E), ALU.mult)
        else:
            ins = nc.vector.tensor_copy(r["g"], scores)
        ins.then_inc(self.misc_drained.sem, 1)
        dve.wait_ge(*self.misc_drained(n + 1))
        apart(dve, k)
        for t in range(CH):
            ins = nc.vector.max(r["best"][:, t, :], r["g"][:, t, :])
        order.mark(ins)
        order.wait()
        apart(dve, k)
        for t in range(CH):
            ins = nc.vector.max_index(r["place"][:, t, :], r["best"][:, t, :], r["g"][:, t, :])
        order.mark(ins)
        if self.kind == "softmax":
            order.mark(nc.vector.tensor_tensor(r["d"][:, :, 0:E], r["g"], r["best"][:, :, 0:1].to_broadcast([P, CH, E]),
                                               ALU.subtract))
        nc.vector.tensor_tensor(r["d"][:, :, E:E + 1], r["best"][:, :, 1:2], r["best"][:, :, 0:1], ALU.subtract)\
            .then_inc(self.shifted.sem, 1)
        order.wait()
        order.mark(nc.vector.tensor_copy(r["placef"], r["place"][:, :, 0:2]))
        order.wait()
        iota = spread(k.consts[:, C_IOTA:C_IOTA + E], 1, CH)
        for j in range(2):
            ins = nc.vector.tensor_tensor(r["is"][:, j], iota, r["placef"][:, :, j:j + 1].to_broadcast([P, CH, E]),
                                          ALU.is_equal)
        order.mark(ins)
        dve.wait_ge(*self.exps(c + 1))
        if self.kind == "softmax":
            order.mark(nc.vector.tensor_reduce(r["z"], r["ex"][:, :, 0:E], AX.X, ALU.add))
        else:
            order.mark(nc.vector.tensor_scalar(r["z"], r["ex"][:, :, E], 1.0, None, ALU.add))
        order.wait()
        order.mark(nc.vector.reciprocal(r["rz"], r["z"]))
        order.wait()
        order.mark(nc.vector.tensor_scalar(r["p"][:, 0], r["rz"], self.gate, None, ALU.mult))
        order.wait()
        order.mark(nc.vector.tensor_tensor(r["p"][:, 1], r["p"][:, 0], r["ex"][:, :, E], ALU.mult))
        order.wait()
        for j in range(2):
            ins = nc.vector.tensor_tensor(r["part"][:, j], r["is"][:, j], spread(r["p"][:, j], 2, E), ALU.mult)
        order.mark(ins)
        order.wait()
        nc.vector.tensor_tensor(r["comb"], r["part"][:, 0], r["part"][:, 1], ALU.add)\
            .then_inc(self.comb_ready.sem, 1)
        dve.wait_ge(*self.comb_ready(c + 1))
        order.mark(nc.vector.tensor_copy(k.comb[:, bass.ds(c * CH, CH), :], r["comb"]))

    def vector_bias(self, dve, order, c):
        k, nc = self.k, self.k.nc
        n = self.m * (c + 1)
        dve.wait_ge(*self.misc_full(n))
        x = k.x[:, bass.ds(c * CH, CH), :]
        nc.vector.tensor_tensor(x, x, k.misc[:].rearrange("p (t d) -> p t d", t=CH), ALU.add)\
            .then_inc(self.misc_drained.sem, 1)

    def vector_add(self, dve, order, c, e):
        k, nc = self.k, self.k.nc
        n = c * E + e
        if self.kind == "gated":
            for f in range(self.nf):
                dve.wait_ge(*self.up_full(4 * n + 2 + f + 1))
                dve.wait_ge(*self.up_drained(2 * n + f + 1))
                nc.vector.tensor_tensor(k.shared[:, e % 2, f * CW:(f + 1) * CW],
                                        k.shared[:, e % 2, (2 + f) * CW:(3 + f) * CW], k.scores[:, 2 + f, :],
                                        ALU.mult).then_inc(self.hidden_done.sem, 1)

    def vector_out(self, dve, order, c, e):
        k, nc = self.k, self.k.nc
        n = c * E + e
        dve.wait_ge(*self.down_full(n + 1))
        if e:
            dve.wait_ge(*self.down_drained(n))
        for t in range(CH):
            x = k.x[:, bass.ds(c * CH + t, 1), :]
            ins = nc.vector.scalar_tensor_tensor(
                out=x, in0=k.probs_ps[:, e % 2, t * P:(t + 1) * P].unsqueeze(1),
                scalar=k.comb[:, bass.ds(c * CH + t, 1), e:e + 1], in1=x, op0=ALU.mult, op1=ALU.add)
        ins.then_inc(self.down_drained.sem, 1)

    def vector_step(self, dve, order, c, prepare):
        order.wait()
        dve.wait_ge(*self.misc_drained(self.m * (c + 1)))
        gated = self.kind == "gated"
        for e in range(E):
            if gated:
                self.vector_add(dve, order, c, e)
            self.vector_out(dve, order, c, e)
            if prepare:
                if e == 0:
                    self.vector_stats(dve, order, c + 1)
                if e == 1:
                    self.vector_scale(dve, order, c + 1)
                if e == 3:
                    self.vector_xnt(dve, order, c + 1)
                if e == 4:
                    self.vector_route(dve, order, c + 1)
                if e == 7 and not gated:
                    self.vector_bias(dve, order, c + 1)

    def vector(self, dve, order):
        dve.wait_ge(*self.before.x_written)
        dve.wait_ge(*self.k.small_ready)
        order.wait()
        self.vector_stats(dve, order, 0)
        self.vector_scale(dve, order, 0)
        self.vector_xnt(dve, order, 0)
        self.vector_route(dve, order, 0)
        if self.kind != "gated":
            self.vector_bias(dve, order, 0)
        marks = {"cosine": 14, "softmax": 12, "gated": 12}[self.kind]
        with self.k.nc.vector.Fori(0, NC - 1) as c, order.turns(c, NC - 1, marks):
            self.vector_step(dve, order, c, True)
        self.vector_step(dve, order, NC - 1, False)


    def scalar_prepare(self, act, c):
        k, nc, r = self.k, self.k.nc, self.r
        n = self.m * c
        act.wait_ge(*self.misc_full(n + 1))
        act.wait_ge(*self.xnt_ready(c))
        if self.kind == "gated":
            nc.scalar.activation(k.xnt_stage[:], k.misc[:], ACT.Identity, bias=self.affine[:, 1:2],
                                 scale=self.affine[:, 0:1]).then_inc(self.misc_drained.sem, 1)
        else:
            nc.scalar.activation(k.xnt_stage[:], k.misc[:], ACT.Copy).then_inc(self.misc_drained.sem, 1)
        if self.kind == "cosine":
            act.wait_ge(*self.misc_full(n + 2))
            for t in range(CH):
                ins = nc.scalar.activation(r["squares"][:, t, :], k.misc[:, t * P:(t + 1) * P], ACT.Square,
                                           accum_out=r["ss"][:, t:t + 1])
            ins.then_inc(self.misc_drained.sem, 1)

    def scalar_comb(self, act, c):
        k, nc = self.k, self.k.nc
        act.wait_ge(*self.misc_full(self.m * c + self.m - 1))
        nc.scalar.activation(self.r["comb_t"][0:E, :], k.misc[0:E, :], ACT.Copy).then_inc(self.misc_drained.sem, 1)

    def scalar_hidden(self, act, c, e):
        k, nc = self.k, self.k.nc
        n = c * E + e
        act.wait_ge(*self.down_full(n - 1))
        for f in range(self.nf):
            act.wait_ge(*self.up_full(4 * n + f + 1))
            if self.kind == "gated":
                nc.scalar.activation(k.shared[:, e % 2, (2 + f) * CW:(3 + f) * CW], k.scores[:, f, :], ACT.Silu)\
                    .then_inc(self.up_drained.sem, 1)
            else:
                nc.scalar.activation(k.shared[:, e % 2, f * CW:(f + 1) * CW], k.scores[:, f, :],
                                     ACT.Gelu if self.kind == "cosine" else ACT.Relu, bias=self.b1[:, e, f:f + 1])\
                    .then_inc(self.up_drained.sem, 1)

    def scalar_step(self, act, c, prepare):
        for e in range(E):
            self.scalar_hidden(act, c, e)
            if prepare:
                if e == 3:
                    self.scalar_prepare(act, c + 1)
                if e == 6 and self.kind != "gated":
                    self.scalar_comb(act, c + 1)

    def scalar(self, act, order):
        act.wait_ge(*self.k.small_ready)
        self.scalar_prepare(act, 0)
        if self.kind != "gated":
            self.scalar_comb(act, 0)
        with self.k.nc.scalar.Fori(0, NC - 1) as c:
            self.scalar_step(act, c, True)
        self.scalar_step(act, NC - 1, False)


    def gpsimd_prepare(self, pool, order, c):
        k, nc, r = self.k, self.k.nc, self.r
        k.ln_pool(pool, order, CH, self.stats, self.rstd, c + 1)
        if self.kind == "cosine":
            pool.wait_ge(*self.misc_drained(self.m * c + 2))
            nc.gpsimd.tensor_tensor(r["norm"], r["ss"], k.consts[:, C_HALF:C_HALF + CH], ALU.pow)\
                .then_inc(self.norms.sem, 1)
        pool.wait_ge(*self.shifted(c + 1))
        first = 0 if self.kind == "softmax" else E
        nc.gpsimd.tensor_tensor(r["ex"][:, :, first:], k.consts[:, C_E:C_E + CH * (E + 1)].rearrange(
            "p (t e) -> p t e", t=CH)[:, :, first:], r["d"][:, :, first:], ALU.pow).then_inc(self.exps.sem, 1)

    def gpsimd(self, pool, order):
        self.gpsimd_prepare(pool, order, 0)
        with self.k.nc.gpsimd.Fori(1, NC) as c, order.turns(c - 1, NC - 1, 1):
            self.gpsimd_prepare(pool, order, c)


    def sync(self, sp):
        k, ins = self.k, self.k.ins
        if self.weights_free:
            sp.wait_ge(*self.weights_free)
        for h in range(2):
            half = slice(h * E // 2, (h + 1) * E // 2)
            sp.dma_start(k.w_up[:, half, :], ins[self.prefix + "up"][:, half, :]).then_inc(self.loaded[h].sem, 16)
            sp.dma_start(k.w_down[:, half, 0:self.nf, :], ins[self.prefix + "down"][:, half, :, :])\
                .then_inc(self.loaded[h].sem, 16)


class DenseLayer:

    def __init__(self, core, gate, before):
        self.k, self.gate, self.before = core, gate, before
        c = core.count
        self.misc_full, self.misc_drained = c("misc_full", NC), c("misc_drained", NC)
        self.up_full, self.up_drained = c("up_full", NC * 4), c("up_drained", NC * 4)
        self.hidden_done = c("hidden_done", NC * 4)
        self.down_full, self.down_drained = c("down_full", NC), c("down_drained", NC)
        self.stats, self.rstd, self.normed = (c(f"ln_{n}", NC) for n in ("stats_done", "rstd_done", "normed"))
        self.others = [c(n, 0) for n in ("scores_drained", "probs_drained")]
        self.x_written = self.down_drained(NC)

    def tensor(self, pe):
        k, nc = self.k, self.k.nc
        for drained in self.others + [self.up_drained, self.down_drained]:
            pe.wait_ge(*drained(0))

        def transpose(c):
            pe.wait_ge(*self.misc_drained(c))
            pe.wait_ge(*self.normed(c + 1))
            for t in range(CH):
                ins = nc.tensor.transpose(k.misc[:, t * P:(t + 1) * P], k.xn[:, t, :], k.ident[:])
            ins.then_inc(self.misc_full.sem, 1)

        def up(c):
            pe.wait_ge(*self.misc_drained(c + 1))
            for f in range(4):
                pe.wait_ge(*self.up_drained(4 * c + f - 3))
                nc.tensor.matmul(k.scores[:, f, :], k.l1_up[:, f * P:(f + 1) * P], k.xnt_stage[:],
                                 start=True, stop=True).then_inc(self.up_full.sem, 1)

        def down(c):
            pe.wait_ge(*self.down_drained(c))
            pe.wait_ge(*self.hidden_done(4 * (c + 1)))
            for t in range(CH):
                for f in range(4):
                    ins = nc.tensor.matmul(k.probs_ps[:, 0, t * P:(t + 1) * P],
                                           k.shared[:, 1, f * CW + t * P:f * CW + (t + 1) * P], k.l1_down[:, f, :],
                                           start=(f == 0), stop=(f == 3))
            ins.then_inc(self.down_full.sem, 1)

        transpose(0)
        with nc.tensor.Fori(0, NC - 1) as c:
            up(c)
            transpose(c + 1)
            down(c)
        up(NC - 1)
        down(NC - 1)

    def vector(self, dve, order):
        k, nc = self.k, self.k.nc
        dve.wait_ge(*self.before.x_written)
        order.wait()

        def normalise(c):
            src = k.x[:, bass.ds(c * CH, CH), :]
            k.ln_vector_stats(dve, order, src, CH, self.stats, c)
            dve.wait_ge(*self.misc_full(c))
            k.ln_vector_scale(dve, src, CH, self.rstd, self.normed, c + 1)

        def hidden(c):
            dve.wait_ge(*self.down_full(c))
            for f in range(4):
                dve.wait_ge(*self.up_drained(4 * c + f + 1))
                r = k.shared[:, 0, f * CW:(f + 1) * CW]
                nc.vector.tensor_tensor(k.shared[:, 1, f * CW:(f + 1) * CW], r, r, ALU.mult)\
                    .then_inc(self.hidden_done.sem, 1)

        def add(c):
            dve.wait_ge(*self.down_full(c + 1))
            x = k.x[:, bass.ds(c * CH, CH), :]
            nc.vector.scalar_tensor_tensor(out=x, in0=k.probs_ps[:, 0, :].rearrange("p (t d) -> p t d", t=CH),
                                           scalar=self.gate, in1=x, op0=ALU.mult, op1=ALU.add)\
                .then_inc(self.down_drained.sem, 1)

        normalise(0)
        with nc.vector.Fori(0, NC - 1) as c, order.turns(c, NC - 1, 1):
            hidden(c)
            normalise(c + 1)
            add(c)
        hidden(NC - 1)
        add(NC - 1)

    def scalar(self, act, order):
        k, nc = self.k, self.k.nc

        def prepare(c):
            act.wait_ge(*self.misc_full(c + 1))
            act.wait_ge(*self.up_full(4 * c))
            nc.scalar.activation(k.xnt_stage[:], k.misc[:], ACT.Copy).then_inc(self.misc_drained.sem, 1)

        def relu(c):
            act.wait_ge(*self.hidden_done(4 * c))
            for f in range(4):
                act.wait_ge(*self.up_full(4 * c + f + 1))
                nc.scalar.activation(k.shared[:, 0, f * CW:(f + 1) * CW], k.scores[:, f, :], ACT.Relu)\
                    .then_inc(self.up_drained.sem, 1)

        prepare(0)
        with nc.scalar.Fori(0, NC - 1) as c:
            relu(c)
            prepare(c + 1)
        relu(NC - 1)

    def gpsimd(self, pool, order):
        with self.k.nc.gpsimd.Fori(0, NC) as c, order.turns(c, NC, 1):
            self.k.ln_pool(pool, order, CH, self.stats, self.rstd, c + 1)

    def sync(self, sp):
        pass


class AttentionMemory:

    def __init__(self, core):
        nc, self.core = core.nc, core

        def sb(name, shape, dt=F32):
            return core.ctx.enter_context(nc.sbuf_tensor(name, shape, dt))

        self.w = sb("attn_w", [P, 4 * 1024])
        self.row = sb("attn_row", [1, 3, P])
        self.bias = sb("attn_bias", [P, 2 * NG + 2])
        self.split_bias = sb("attn_split_bias", [P, 2, NG])
        self.zero_bias = sb("attn_zero_bias", [P, 1])
        self.ctx_t = sb("attn_ctx", [P, 2, S])
        self.xnt = core.xnt[:, 0:2 * S].rearrange("p (s t) -> p s t", s=2)
        self.work = sb("attn_work", [P, 5 * NG * S])
        work = self.work[:].rearrange("p (j g s) -> p j g s", j=5, g=NG)
        self.q = sb("attn_q", [P, 2, NG, S], F32R)
        mask_i = self.work[:, 0:2 * NG * S].bitcast(I32).rearrange("p (s l t k) -> p s l t k", s=2, l=2, t=TPB)
        core.causal_raw = self.work[:, 0:4 * S].rearrange("p (l t k) -> p l t k", l=2, t=TPB)
        self.k = work[:, 2].bitcast(F32R)
        self.k_own = sb("attn_k_own", [P, 2, NG, GH, S], F32R)
        self.split = work[:, 3].bitcast(F32R)
        self.v = sb("attn_v", [P, 2, TPB, H, Q32])
        self.neg_max = sb("attn_neg_max", [P, TPB, GH, NG])
        self.max_t = sb("attn_max_t", [H, S], F32R)
        self.u = work[:, 4]
        self.rsum = sb("attn_rsum", [P, 2, TPB, GH])
        self.mixed = sb("attn_mixed", [P, TPB, D])
        self.mixed_t = sb("attn_mixed_t", [P, S])
        self.mask_raw = {"integer": mask_i, "boolean": sb("attn_mask_raw", [P, 2, 2, TPB, S], U8)}
        self.mask = sb("attn_mask", [P, 2, 2, TPB, S], BF16)
        self.zeroed = core.count("attn_zeroed", 1)
        self.weights_loaded = core.count("attn_weights_loaded", 0)

    def clear(self, pool):
        nc, k = self.core.nc, self.core
        pool.wait_ge(k.loaded_consts, 32)
        pool.wait_ge(k.loaded_causal, 16)
        nc.gpsimd.tensor_copy(k.ident_bf[:], k.ident[:])
        nc.gpsimd.tensor_copy(k.masks_causal[:], k.causal_raw)
        nc.gpsimd.memset(self.k_own[:].bitcast(F32), 0.0)
        nc.gpsimd.memset(self.zero_bias[:], 0.0)
        nc.gpsimd.memset(self.v[:, :, :, :, HD + 1:], 0.0)
        nc.gpsimd.memset(self.v[:, :, :, :, HD:HD + 1], 1.0).then_inc(self.zeroed.sem, 1)


class Step:

    def __init__(self, b):
        self.b = b
        peeled = isinstance(b, int)
        self.ends = not peeled or b > 0
        self.leads = not peeled or b + 1 < B
        self.prepares = not peeled or b + 2 < B
        self.makes = dict(v=self.leads, u1=self.ends, xnt=self.prepares, mixed=self.ends, out=self.ends,
                          u0=not peeled or b < B, max=self.leads)
        order = [name for name, made in self.makes.items() if made]
        base = 4 if peeled and b == 0 else 1 + 7 * b
        if peeled and b >= B - 1:
            base = 1 + 7 * (B - 1) - 1
        if peeled and b >= B:
            base = base + 4
        self.misc = {name: base + n for n, name in enumerate(order)}
        self.misc_start = base
        self.scores = 12 + 10 * b
        self.keys, self.queries = self.scores + 6, self.scores + 9

    def maxima(self, g, qt):
        n = 2 * g + qt + (1 if g == 3 and self.prepares else 0)
        return self.scores + n, n % 2


class NarrowAttention:

    def __init__(self, core, memory, kind, prefix, gate, before):
        self.k, self.m, self.kind, self.prefix, self.gate, self.before = core, memory, kind, prefix, gate, before
        c = core.count
        uses = 7 * B
        self.misc_full, self.misc_drained = c("misc_full", uses), c("misc_drained", uses)
        self.scores_full, self.scores_drained = c("scores_full", 10 * B), c("scores_drained", 10 * B)
        self.probs_full, self.probs_drained = c("probs_full", 16 * B), c("probs_drained", 16 * B)
        self.mixed_full, self.mixed_drained = c("mixed_full", 4 * B), c("mixed_drained", 2 * B)
        self.stats, self.rstd, self.normed = (c(f"ln_{n}", B) for n in ("stats_done", "rstd_done", "normed"))
        self.split_hi = c("attn_split_hi", 2 * B)
        self.keys_spread = [c(f"attn_keys_spread{h}", 64 * B) for h in range(2)]
        self.max_spread = c("attn_max_spread", 16 * B)
        masked = kind != "causal"
        self.ctx_loaded = [c(f"attn_ctx_loaded{s}", 16 * B // 2 if masked else 0) for s in range(2)]
        self.mask_loaded = [c(f"attn_mask_loaded{s}", 16 * B // 2 if masked else 0) for s in range(2)]
        self.mask_q, self.mask_k = (c(f"attn_mask_{n}", B if masked else 0) for n in "qk")
        self.weights_loaded = c("attn_weights_loaded", 48)
        self.free = [c(n, 0) for n in ("up_drained", "down_drained")]
        self.weights_free, core.attention_done = core.attention_done, self.misc_drained(uses)
        self.x_written = self.misc_drained(uses)
        self.biased = kind == "boolean"
        w = memory.w
        self.wq = w[:, 0:512].rearrange("p (g n) -> p g n", g=NG)
        self.wk = w[:, 512:1024].rearrange("p (g n) -> p g n", g=NG)
        self.wv, self.wo = w[:, 1024:1152], w[:, 1152:1280]
        self.bias = memory.bias[:, 0:2 * NG].rearrange("p (w g) -> p w g", w=2)
        self.affine = memory.bias[:, 2 * NG:2 * NG + 2]
        self.src = core.y if kind == "causal" else core.x

    def source(self, s):
        return self.m.xnt[:, s, :] if self.kind == "causal" else self.m.ctx_t[:, s, :]

    def masks(self, s, layout, t):
        masks = self.k.masks_causal[:, layout, t, :] if self.kind == "causal" else self.m.mask[:, s, layout, t, :]
        return spread(masks, 1, 2)


    def t_fill_scores(self, pe, n):
        if not isinstance(n, int) or n >= 2:
            pe.wait_ge(*self.scores_drained(n - 1))

    def t_pass1(self, pe, b, s, use, g, qt):
        k, nc = self.k, self.k.nc
        n, slot = use
        if g % 2 == 0 and qt == 0:
            pe.wait_ge(*self.keys_spread[g // 2](64 * (b + 1)))
        if g == 0 and qt == 0:
            pe.wait_ge(*self.scores_drained(n))
            if self.kind != "causal":
                pe.wait_ge(*self.mask_q(b + 1))
        self.t_fill_scores(pe, n)
        for pair in range(2):
            out = k.scores[:, 2 * slot + pair, :]
            nc.tensor.matmul(out.rearrange("p (i s) -> p i s", i=2), k.ident_bf[:], self.masks(s, 0, qt),
                             start=True, stop=False)
            ins = nc.tensor.matmul(out, self.m.q[:, s, g, qt * P:(qt + 1) * P],
                                   self.m.k_own[:, s, g, 2 * pair:2 * pair + 2, :].rearrange("p i s -> p (i s)"),
                                   start=False, stop=True)
        ins.then_inc(self.scores_full.sem, 1)

    def t_pass2(self, pe, b, s, g, kt):
        k, nc = self.k, self.k.nc
        if g == 0 and kt == 0:
            pe.wait_ge(*self.max_spread(16 * (b + 1)))
            if self.kind != "causal":
                pe.wait_ge(*self.mask_k(b + 1))
        for pair in range(2):
            n = 16 * b + 4 * g + 2 * kt + pair
            pe.wait_ge(*self.probs_drained(n - 1 if (g or kt) else 16 * b))
            out = k.probs_ps[:, pair, :]
            nc.tensor.matmul(out.rearrange("p (i s) -> p i s", i=2), k.ident_bf[:], self.masks(s, 1, kt),
                             start=True, stop=False)
            for i in range(2):
                ins = nc.tensor.matmul(out[:, i * S:(i + 1) * S],
                                       self.m.k_own[:, s, g, 2 * pair + i, kt * P:(kt + 1) * P],
                                       self.m.q[:, s, g, :], start=False, stop=(i == 1))
            ins.then_inc(self.probs_full.sem, 1)

    def t_mix(self, pe, b, s, g):
        k, nc = self.k, self.k.nc
        if g % 2 == 0:
            pe.wait_ge(*self.mixed_drained(2 * b + g // 2))
        pe.wait_ge(*self.probs_drained(16 * b + 4 * g + 4))
        for kt in range(TPB):
            for i in range(GH):
                ins = nc.tensor.matmul(k.mixed[i * Q32:(i + 1) * Q32, (g % 2) * S:(g % 2 + 1) * S],
                                       self.m.v[:, s, kt, g * GH + i, :],
                                       k.shared[:, g % 2, (kt * GH + i) * S:(kt * GH + i + 1) * S],
                                       start=(kt == 0), stop=(kt == TPB - 1), skip_group_check=True)
        ins.then_inc(self.mixed_full.sem, 1)

    def t_xnt(self, pe, b, n):
        k, nc = self.k, self.k.nc
        pe.wait_ge(*self.misc_drained(n))
        pe.wait_ge(*self.normed(b + 1))
        for t in range(TPB):
            ins = nc.tensor.transpose(k.misc[:, t * P:(t + 1) * P], k.xn[:, t, :], k.ident[:])
        ins.then_inc(self.misc_full.sem, 1)

    def t_project(self, pe, w, src, slot, n):
        k, nc = self.k, self.k.nc
        self.t_fill_scores(pe, n)
        for g in range(NG):
            ins = nc.tensor.matmul(k.scores[:, 2 * slot + g // 2, (g % 2) * S:(g % 2 + 1) * S], w[:, g, :], src,
                                   start=True, stop=True)
        ins.then_inc(self.scores_full.sem, 1)

    def t_keys(self, pe, b, s, slot, n, xnt_use):
        if self.kind == "causal":
            pe.wait_ge(*self.misc_drained(xnt_use + 1))
        else:
            pe.wait_ge(*self.ctx_loaded[s](8 * (b - s) + 16))
        self.t_project(pe, self.wk, self.source(s), slot, n)

    def t_queries(self, pe, s, slot, n, xnt_use):
        pe.wait_ge(*self.misc_drained(xnt_use + 1))
        self.t_project(pe, self.wq, self.m.xnt[:, s, :], slot, n)

    def t_values(self, pe, s, n):
        k, nc = self.k, self.k.nc
        pe.wait_ge(*self.misc_drained(n))
        for t in range(TPB):
            if self.biased:
                nc.tensor.matmul(k.misc[:, t * P:(t + 1) * P], self.m.row[:, 0, :], self.m.row[:, 1, :], start=True,
                                 stop=False)
            ins = nc.tensor.matmul(k.misc[:, t * P:(t + 1) * P], self.source(s)[:, t * P:(t + 1) * P], self.wv,
                                   start=not self.biased, stop=True)
        ins.then_inc(self.misc_full.sem, 1)

    def t_max(self, pe, n, drained):
        k, nc = self.k, self.k.nc
        pe.wait_ge(*self.misc_drained(n))
        pe.wait_ge(*self.scores_drained(drained))
        for t in range(TPB):
            ins = nc.tensor.transpose(k.misc[0:H, t * P:(t + 1) * P],
                                      self.m.neg_max[:, t, :, :].rearrange("p i g -> p (i g)"), k.ident[:])
        ins.then_inc(self.misc_full.sem, 1)

    def t_u(self, pe, b, h, n):
        k, nc = self.k, self.k.nc
        pe.wait_ge(*self.misc_drained(n))
        pe.wait_ge(*self.mixed_drained(2 * b + h + 1))
        for g in range(2):
            for t in range(TPB):
                c = (g * TPB + t) * P
                ins = nc.tensor.transpose(k.misc[:, c:c + P], self.m.u[:, 2 * h + g, t * P:(t + 1) * P], k.ident[:])
        ins.then_inc(self.misc_full.sem, 1)

    def t_mixed(self, pe, n):
        k, nc = self.k, self.k.nc
        pe.wait_ge(*self.misc_drained(n))
        for t in range(TPB):
            ins = nc.tensor.transpose(k.misc[:, t * P:(t + 1) * P], self.m.mixed[:, t, :], k.ident[:])
        ins.then_inc(self.misc_full.sem, 1)

    def t_out(self, pe, n):
        k, nc = self.k, self.k.nc
        pe.wait_ge(*self.misc_drained(n))
        bias = self.kind != "integer"
        for t in range(TPB):
            if bias:
                nc.tensor.matmul(k.misc[:, t * P:(t + 1) * P], self.m.row[:, 0, :], self.m.row[:, 2, :], start=True,
                                 stop=False)
            ins = nc.tensor.matmul(k.misc[:, t * P:(t + 1) * P], self.m.mixed_t[:, t * P:(t + 1) * P], self.wo,
                                   start=not bias, stop=True)
        ins.then_inc(self.misc_full.sem, 1)

    def t_step(self, pe, b, s):
        st = Step(b)

        def pass1(g, qt):
            if st.leads:
                self.t_pass1(pe, b + 1, 1 - s, st.maxima(g, qt), g, qt)

        if st.ends:
            self.t_mix(pe, b - 1, 1 - s, 3)
        pass1(0, 0)
        if st.leads:
            self.t_values(pe, 1 - s, st.misc["v"])
        self.t_pass2(pe, b, s, 0, 0)
        pass1(0, 1)
        self.t_pass2(pe, b, s, 0, 1)

        pass1(1, 0)
        if st.ends:
            self.t_u(pe, b - 1, 1, st.misc["u1"])
        self.t_pass2(pe, b, s, 1, 0)
        pass1(1, 1)
        self.t_mix(pe, b, s, 0)
        self.t_pass2(pe, b, s, 1, 1)
        if st.prepares:
            self.t_xnt(pe, b + 2, st.misc["xnt"])

        pass1(2, 0)
        if st.ends:
            self.t_mixed(pe, st.misc["mixed"])
        self.t_pass2(pe, b, s, 2, 0)
        pass1(2, 1)
        self.t_mix(pe, b, s, 1)
        self.t_pass2(pe, b, s, 2, 1)
        if st.prepares:
            self.t_keys(pe, b + 2, s, 0, st.keys, st.misc["xnt"])

        pass1(3, 0)
        if st.ends:
            self.t_out(pe, st.misc["out"])
        self.t_pass2(pe, b, s, 3, 0)
        pass1(3, 1)
        if st.prepares:
            self.t_queries(pe, s, 1, st.queries, st.misc["xnt"])
        self.t_u(pe, b, 0, st.misc["u0"])
        self.t_pass2(pe, b, s, 3, 1)
        if st.leads:
            self.t_max(pe, st.misc["max"], st.scores + 8 + st.prepares)
        self.t_mix(pe, b, s, 2)

    def t_end(self, pe):
        st = Step(B)
        self.t_mix(pe, B - 1, (B - 1) % 2, 3)
        self.t_u(pe, B - 1, 1, st.misc["u1"])
        self.t_mixed(pe, st.misc["mixed"])
        self.t_out(pe, st.misc["out"])

    def steps(self, eng, step):
        step(0, 0)
        with eng.Fori(0, (B - 4) // 2) as i:
            for n in range(2):
                step(2 * i + 1 + n, (1 + n) % 2)
        for b in (B - 3, B - 2, B - 1):
            step(b, b % 2)

    def tensor(self, pe):
        for drained in self.free + [self.scores_drained, self.probs_drained, self.mixed_drained]:
            pe.wait_ge(*drained(0))
        pe.wait_ge(*self.m.zeroed(1))
        pe.wait_ge(*self.weights_loaded(48))
        for b in range(2):
            self.t_xnt(pe, b, b)
            self.t_keys(pe, b, b, 0, 2 * b, b)
            self.t_queries(pe, b, 1, 2 * b + 1, b)
        self.t_values(pe, 0, 2)
        for g in range(NG):
            for qt in range(TPB):
                self.t_pass1(pe, 0, 0, (4 + 2 * g + qt, qt), g, qt)
        self.t_max(pe, 3, 12)
        self.steps(self.k.nc.tensor, lambda b, s: self.t_step(pe, b, s))
        self.t_end(pe)


    def v_stats(self, dve, order, b):
        self.k.ln_vector_stats(dve, order, self.src[:, bass.ds(b * TPB, TPB), :], TPB, self.stats, b)

    def v_scale(self, dve, b):
        self.k.ln_vector_scale(dve, self.src[:, bass.ds(b * TPB, TPB), :], TPB, self.rstd, self.normed, b + 1)

    def v_max(self, dve, use, g, qt):
        k, nc = self.k, self.k.nc
        n, slot = use
        dve.wait_ge(*self.scores_full(n + 1))
        nc.vector.tensor_reduce(self.m.neg_max[:, qt, :, g],
                                k.scores[:, 2 * slot:2 * slot + 2, :].rearrange("p a (i s) -> p (a i) s", i=2),
                                AX.X, ALU.max, negate=True).then_inc(self.scores_drained.sem, 1)

    def v_split(self, dve, which, out, slot, n, nth):
        k, nc = self.k, self.k.nc
        dve.wait_ge(*self.split_hi(nth))
        ps = k.scores[:, 2 * slot:2 * slot + 2, :].rearrange("p a (g s) -> p (a g) s", g=2)
        if self.biased:
            for g in range(NG):
                ins = nc.vector.scalar_tensor_tensor(out=out[:, g, :], in0=ps[:, g, :],
                                                     scalar=self.bias[:, which, g:g + 1],
                                                     in1=self.m.split[:, g, :].bitcast(F32), op0=ALU.add, op1=ALU.add)
        else:
            bias = k.consts[:, C_ONES:C_ONES + 1] if which else self.m.zero_bias[:]
            ins = nc.vector.scalar_tensor_tensor(out=out, in0=ps, scalar=bias, in1=self.m.split.bitcast(F32),
                                                 op0=ALU.add, op1=ALU.add)
        ins.then_inc(self.scores_drained.sem, 1)

    def v_max_t(self, dve, b, n):
        k, nc = self.k, self.k.nc
        dve.wait_ge(*self.misc_full(n + 1))
        if not isinstance(b, int) or b > 0:
            dve.wait_ge(*self.max_spread(16 * b))
        nc.vector.tensor_copy(self.m.max_t[:], k.misc[0:H, 0:S]).then_inc(self.misc_drained.sem, 1)

    def v_u(self, dve, order, h, n):
        k, nc = self.k, self.k.nc
        u = k.misc[:].rearrange("p (g t i r) -> p g t i r", g=2, t=TPB, i=GH)
        dve.wait_ge(*self.misc_full(n + 1))
        order.mark(nc.vector.reciprocal(self.m.rsum[:], u[:, :, :, :, HD]))
        order.wait()
        for t in range(TPB):
            out = self.m.mixed[:, t, :].rearrange("p (g i r) -> p g i r", g=NG, i=GH)[:, 2 * h:2 * h + 2]
            ins = nc.vector.tensor_tensor(out, u[:, :, t, :, 0:HD],
                                          spread(self.m.rsum[:, :, t, :], 3, HD), ALU.mult)
        ins.then_inc(self.misc_drained.sem, 1)

    def v_out(self, dve, b, n):
        k, nc = self.k, self.k.nc
        dve.wait_ge(*self.misc_full(n + 1))
        x = self.src[:, bass.ds(b * TPB, TPB), :]
        ps = k.misc[:, 0:S].rearrange("p (t d) -> p t d", t=TPB)
        if self.kind == "causal":
            ins = nc.vector.tensor_tensor(x, ps, x, ALU.add)
        else:
            ins = nc.vector.scalar_tensor_tensor(out=x, in0=ps, scalar=self.gate, in1=x, op0=ALU.mult, op1=ALU.add)
        ins.then_inc(self.misc_drained.sem, 1)

    def v_keys(self, dve, b, slot, n):
        if not isinstance(b, int) or b > 0:
            for h in range(2):
                dve.wait_ge(*self.keys_spread[h](64 * b))
        self.v_split(dve, 1, self.m.k, slot, n, 2 * b + 1)

    def v_step(self, dve, order, b, s):
        st = Step(b)

        def maxima(g, qt):
            if st.leads:
                self.v_max(dve, st.maxima(g, qt), g, qt)

        maxima(0, 0)
        maxima(0, 1)
        if st.prepares:
            self.v_stats(dve, order, b + 2)
        maxima(1, 0)
        if st.ends:
            self.v_u(dve, order, 1, st.misc["u1"])
        if st.prepares:
            self.v_scale(dve, b + 2)
        maxima(1, 1)
        maxima(2, 0)
        maxima(2, 1)
        if st.prepares:
            self.v_keys(dve, b + 2, 0, st.keys)
        maxima(3, 0)
        if st.ends:
            self.v_out(dve, b - 1, st.misc["out"])
        maxima(3, 1)
        self.v_u(dve, order, 0, st.misc["u0"])
        if st.leads:
            self.v_max_t(dve, b + 1, st.misc["max"])
        if st.prepares:
            dve.wait_ge(*self.probs_full(16 * (b + 1)))
            self.v_split(dve, 0, self.m.q[:, s], 1, st.queries, 2 * b + 6)

    def vector(self, dve, order):
        k = self.k
        dve.wait_ge(*self.before.x_written)
        dve.wait_ge(*self.weights_loaded(48))
        order.wait()
        for b in range(2):
            self.v_stats(dve, order, b)
            if b:
                dve.wait_ge(*self.misc_full(1))
            self.v_scale(dve, b)
            self.v_keys(dve, b, 0, 2 * b)
            self.v_split(dve, 0, self.m.q[:, b], 1, 2 * b + 1, 2 * b + 2)
        for g in range(NG):
            for qt in range(TPB):
                self.v_max(dve, (4 + 2 * g + qt, qt), g, qt)
        self.v_max_t(dve, 0, 3)
        self.v_step(dve, order, 0, 0)
        with k.nc.vector.Fori(0, (B - 4) // 2) as i, order.turns(i, (B - 4) // 2, 6):
            for n in range(2):
                self.v_step(dve, order, 2 * i + 1 + n, (1 + n) % 2)
        for b in (B - 3, B - 2, B - 1):
            self.v_step(dve, order, b, b % 2)
        st = Step(B)
        self.v_u(dve, order, 1, st.misc["u1"])
        self.v_out(dve, B - 1, st.misc["out"])


    def s_exp(self, act, b, g, kt):
        k, nc = self.k, self.k.nc
        if kt == 0:
            act.wait_ge(*self.mixed_full(4 * b + max(g - 1, 0)))
        for pair in range(2):
            act.wait_ge(*self.probs_full(16 * b + 4 * g + 2 * kt + pair + 1))
            c = (kt * GH + 2 * pair) * S
            nc.scalar.activation(k.shared[:, g % 2, c:c + 2 * S], k.probs_ps[:, pair, :], ACT.Exp,
                                 scale=float(1 / np.sqrt(HD))).then_inc(self.probs_drained.sem, 1)

    def s_u(self, act, b, h):
        k, nc = self.k, self.k.nc
        act.wait_ge(*self.mixed_full(4 * b + 2 * h + 2))
        nc.scalar.activation(self.m.u[:, 2 * h:2 * h + 2, :].rearrange("p g s -> p (g s)"), k.mixed[:], ACT.Copy)\
            .then_inc(self.mixed_drained.sem, 1)

    def s_xnt(self, act, s, n):
        k, nc = self.k, self.k.nc
        act.wait_ge(*self.misc_full(n + 1))
        if self.kind == "causal":
            ins = nc.scalar.activation(self.m.xnt[:, s, :], k.misc[:, 0:S], ACT.Identity, bias=self.affine[:, 1:2],
                                       scale=self.affine[:, 0:1])
        else:
            ins = nc.scalar.activation(self.m.xnt[:, s, :], k.misc[:, 0:S], ACT.Copy)
        ins.then_inc(self.misc_drained.sem, 1)

    def s_split(self, act, which, slot, n):
        k, nc = self.k, self.k.nc
        act.wait_ge(*self.scores_full(n + 1))
        act.wait_ge(*self.scores_drained(n))
        c = k.consts[:, C_SPLIT + which:C_SPLIT + which + 1]
        ps = k.scores[:, 2 * slot:2 * slot + 2, :].rearrange("p a (g s) -> p (a g) s", g=2)
        if self.biased:
            for g in range(NG):
                ins = nc.scalar.activation(self.m.split[:, g, :], ps[:, g, :], ACT.Identity, scale=c,
                                           bias=self.m.split_bias[:, which, g:g + 1])
        else:
            ins = nc.scalar.activation(self.m.split, ps, ACT.Identity, scale=c, bias=self.m.zero_bias[:])
        ins.then_inc(self.split_hi.sem, 1)

    def s_values(self, act, s, n):
        k, nc = self.k, self.k.nc
        act.wait_ge(*self.misc_full(n + 1))
        nc.scalar.activation(self.m.v[:, s, :, :, 0:HD],
                             k.misc[:, 0:S].rearrange("p (t h d) -> p t h d", t=TPB, h=H), ACT.Copy)\
            .then_inc(self.misc_drained.sem, 1)

    def s_mixed(self, act, n):
        k, nc = self.k, self.k.nc
        act.wait_ge(*self.misc_full(n + 1))
        nc.scalar.activation(self.m.mixed_t[:], k.misc[:, 0:S], ACT.Copy).then_inc(self.misc_drained.sem, 1)

    def s_step(self, act, b, s):
        st = Step(b)
        if st.ends:
            self.s_u(act, b - 1, 1)
        if st.leads:
            self.s_values(act, 1 - s, st.misc["v"])
        for kt in range(TPB):
            self.s_exp(act, b, 0, kt)
        for kt in range(TPB):
            self.s_exp(act, b, 1, kt)
        if st.prepares:
            self.s_xnt(act, s, st.misc["xnt"])
        if st.ends:
            self.s_mixed(act, st.misc["mixed"])
        self.s_exp(act, b, 2, 0)
        self.s_u(act, b, 0)
        self.s_exp(act, b, 2, 1)
        if st.prepares:
            self.s_split(act, 1, 0, st.keys)
        self.s_exp(act, b, 3, 0)
        if st.prepares:
            self.s_split(act, 0, 1, st.queries)
        self.s_exp(act, b, 3, 1)

    def scalar(self, act, order):
        k, nc = self.k, self.k.nc
        act.wait_ge(*self.m.zeroed(1))
        act.wait_ge(*self.weights_loaded(48))
        if self.biased:
            for which in range(2):
                order.mark(nc.scalar.activation(self.m.split_bias[:, which, :], self.bias[:, which, :], ACT.Identity,
                                                scale=k.consts[:, C_SPLIT + which:C_SPLIT + which + 1],
                                                bias=self.m.zero_bias[:]))
            order.wait()
        for b in range(2):
            self.s_xnt(act, b, b)
            self.s_split(act, 1, 0, 2 * b)
            self.s_split(act, 0, 1, 2 * b + 1)
        self.s_values(act, 0, 2)
        self.steps(nc.scalar, lambda b, s: self.s_step(act, b, s))
        self.s_u(act, B - 1, 1)
        self.s_mixed(act, Step(B).misc["mixed"])


    def g_mask(self, s, layout):
        nc, out, raw = self.k.nc, self.m.mask[:, s, layout], self.m.mask_raw[self.kind][:, s, layout]
        if self.kind == "integer":
            return nc.gpsimd.tensor_scalar(out, raw, 0, MASKED, ALU.is_equal, ALU.mult)
        return nc.gpsimd.tensor_scalar(out, raw, MASKED, None, ALU.mult)

    def g_masks(self, pool, b, s, queries_used, keys_used):
        if self.kind == "causal":
            return
        pool.wait_ge(*self.mask_loaded[s](8 * (b - s) + 16))
        pool.wait_ge(*queries_used)
        apart(pool, self.k)
        self.g_mask(s, 0).then_inc(self.mask_q.sem, 1)
        pool.wait_ge(*keys_used)
        apart(pool, self.k)
        self.g_mask(s, 1).then_inc(self.mask_k.sem, 1)

    def gpsimd(self, pool, order):
        k, nc = self.k, self.k.nc
        for b in range(2):
            self.g_masks(pool, b, b, self.scores_full(0), self.probs_full(0))
            k.ln_pool(pool, order, TPB, self.stats, self.rstd, b + 1)
        with nc.gpsimd.Fori(0, (B - 2) // 2) as i, order.turns(i, (B - 2) // 2, 2):
            for s in range(2):
                b = 2 * i + s
                k.ln_pool(pool, order, TPB, self.stats, self.rstd, b + 3)
                self.g_masks(pool, b + 2, s, self.scores_full(Step(b).scores), self.probs_full(16 * (b + 1)))


    def d_batch(self, sp, b, s):
        k, ins = self.k, self.k.ins
        if self.kind != "causal":
            sp.dma_start(self.m.ctx_t[:, s, :], ins["ctx_t"][:, bass.ds(b * S, S)]).then_inc(self.ctx_loaded[s].sem, 16)
            sp.dma_start(self.m.mask_raw[self.kind][:, s].rearrange("p l t s -> p (l t s)"),
                         ins[self.prefix + "mask"][bass.ds(b * P, P), :]).then_inc(self.mask_loaded[s].sem, 16)

    def d_keys(self, sp, s, h):
        for i in range(GH):
            r, g = slice(i * Q32, (i + 1) * Q32), slice(2 * h, 2 * h + 2)
            sp.dma_start(self.m.k_own[r, s, g, i, :].bitcast(F32), self.m.k[r, g, :].bitcast(F32))\
                .then_inc(self.keys_spread[h].sem, 16)

    def d_max(self, sp, s, n):
        sp.wait_ge(*self.misc_drained(n + 1))
        apart(sp, self.k)
        sp.dma_start(self.m.q[0:P:Q32, s, :, :].bitcast(F32), self.m.max_t[:].bitcast(F32))\
            .then_inc(self.max_spread.sem, 16)

    def d_step(self, sp, b, s):
        st = Step(b)
        if st.prepares:
            sp.wait_ge(*self.misc_full(st.misc_start))
            apart(sp, self.k)
            if self.kind != "causal":
                sp.wait_ge(*self.mask_k(b + 1))
                apart(sp, self.k)
            self.d_batch(sp, b + 2, s)
            sp.wait_ge(*self.scores_drained(st.keys + 1))
            apart(sp, self.k)
            self.d_keys(sp, s, 0)
        if st.leads:
            self.d_max(sp, 1 - s, st.misc["max"])
        if st.prepares:
            sp.wait_ge(*self.probs_full(16 * (b + 1)))
            apart(sp, self.k)
            self.d_keys(sp, s, 1)

    def sync(self, sp):
        k, ins, m = self.k, self.k.ins, self.m
        if self.weights_free:
            sp.wait_ge(*self.weights_free)
        sp.dma_start(m.w[:, 0:1280], ins[self.prefix + "w"]).then_inc(self.weights_loaded.sem, 16)
        sp.dma_start(m.row[:], ins[self.prefix + "row"]).then_inc(self.weights_loaded.sem, 16)
        sp.dma_start(m.bias[:], ins[self.prefix + "bias"]).then_inc(self.weights_loaded.sem, 16)
        sp.wait_ge(*self.m.zeroed(1))
        for b in range(2):
            self.d_batch(sp, b, b)
        for b in range(2):
            sp.wait_ge(*self.scores_drained(2 * b + 1))
            for h in range(2):
                self.d_keys(sp, b, h)
        self.d_max(sp, 0, 3)
        with k.nc.sync.Fori(0, (B - 2) // 2) as i:
            for s in range(2):
                self.d_step(sp, 2 * i + s, s)
        self.d_step(sp, B - 2, 0)


class WideAttention:

    PAIRS = H // 2

    def __init__(self, core, memory, prefix, gate, before):
        self.k, self.m, self.prefix, self.gate, self.before = core, memory, prefix, gate, before
        c, units = core.count, B * self.PAIRS
        uses = 18 * B
        self.misc_full, self.misc_drained = c("misc_full", uses), c("misc_drained", uses)
        self.scores_full, self.scores_drained = c("scores_full", 4 * units), c("scores_drained", 4 * units)
        self.max_done = c("wide_max_done", 4 * units)
        self.probs_ready = c("wide_probs_ready", units)
        self.probs_full, self.probs_drained = c("probs_full", 3 * units), c("probs_drained", 3 * units)
        self.mixed_full, self.mixed_drained = c("mixed_full", units), c("mixed_drained", units)
        self.stats, self.rstd, self.normed = (c(f"ln_{n}", B) for n in ("stats_done", "rstd_done", "normed"))
        self.ctx_loaded = c("wide_ctx_loaded", 16 * B)
        self.weights_loaded = c("attn_weights_loaded", 80)
        self.free = [c(n, 0) for n in ("up_drained", "down_drained")]
        self.weights_free, core.attention_done = core.attention_done, self.misc_drained(uses)
        self.x_written = self.misc_drained(uses)
        nc = core.nc

        def sb(name, shape):
            return core.ctx.enter_context(nc.sbuf_tensor(name, shape, F32))

        w = memory.w[:].rearrange("p (j f n) -> p j f n", j=4, n=P)
        self.wq, self.wk, self.wv, self.wo = (w[:, j] for j in range(4))
        y = core.y[:].rearrange("p (j f) n -> p j f n", j=2)
        self.mem_k, self.mem_v = y[:, 0], y[:, 1]
        self.v_bias = sb("wide_v_bias", [P, 8, P])
        self.bias = sb("wide_bias", [P, 3, 8])
        work = memory.work[:].rearrange("p (n s) -> p n s", s=S)
        self.mixed_t = work[:, 0:8]
        self.q, self.key = work[:, 8:10], work[:, 10:12]
        self.v = work[:, 12:14].rearrange("p n (t d) -> p n t d", t=TPB)
        self.probs_t = work[:, 14:20].rearrange("p (t j) s -> p t j s", j=2)
        self.probs = core.shared[:].rearrange("p a b -> p (a b)")[:, 0:2 * 4 * 384]\
            .rearrange("p (s r k) -> p s r k", s=2, r=4)
        self.neg_max = sb("wide_neg_max", [P, 2, 4])
        self.sum = sb("wide_sum", [P, 2, 4])
        self.rsum = sb("wide_rsum", [P, 4])
        self.xnt = core.xnt[:, 0:S]
        self.ctx_t = memory.ctx_t[:, 0, :]

    def use(self, b, p, name):
        first = 3 + 18 * b - (0 if isinstance(b, int) and b == 0 else 1)
        out = 0 if isinstance(b, int) and b == 0 else 1
        if name == "out":
            return first + 2
        place = 2 * p + (out if p else 0)
        if p == self.PAIRS - 1:
            return first + place + {"xnt": 0, "qk": 1, "v": 2}[name]
        return first + place + {"qk": 0, "v": 1}[name]


    def t_xnt(self, pe, b, n):
        k, nc = self.k, self.k.nc
        pe.wait_ge(*self.misc_drained(n))
        pe.wait_ge(*self.normed(b + 1))
        for t in range(TPB):
            ins = nc.tensor.transpose(k.misc[:, t * P:(t + 1) * P], k.xn[:, t, :], k.ident[:])
        ins.then_inc(self.misc_full.sem, 1)

    def t_qk(self, pe, b, p, n):
        k, nc = self.k, self.k.nc
        pe.wait_ge(*self.misc_drained(n))
        if p == 0:
            pe.wait_ge(*self.ctx_loaded(16 * (b + 1)))
        nc.tensor.matmul(k.misc[:, 0:S], self.wq[:, p, :], self.xnt, start=True, stop=True)
        nc.tensor.matmul(k.misc[:, S:2 * S], self.wk[:, p, :], self.ctx_t, start=True, stop=True)\
            .then_inc(self.misc_full.sem, 1)

    def t_v(self, pe, p, n):
        k, nc = self.k, self.k.nc
        pe.wait_ge(*self.misc_drained(n))
        for t in range(TPB):
            ins = nc.tensor.matmul(k.misc[:, t * P:(t + 1) * P], self.ctx_t[:, t * P:(t + 1) * P], self.wv[:, p, :],
                                   start=True, stop=True)
        ins.then_inc(self.misc_full.sem, 1)

    def t_scores(self, pe, b, p, n):
        k, nc, u = self.k, self.k.nc, self.PAIRS * b + p
        if n == 0:
            pe.wait_ge(*self.misc_drained(self.qk_use(b, p) + 1))
        r = slice(n // 2 * DK2, (n // 2 + 1) * DK2)
        if not isinstance(u, int) or u > 0:
            pe.wait_ge(*self.scores_drained(4 * u + n - 3))
        q = self.q[r, p % 2, n % 2 * P:(n % 2 + 1) * P]
        nc.tensor.matmul(k.scores[:, n, 0:S], q, self.key[r, p % 2, :], start=True, stop=True)
        nc.tensor.matmul(k.scores[:, n, S:S + MEM], q, self.mem_k[r, p, :], start=True, stop=True)\
            .then_inc(self.scores_full.sem, 1)

    def t_transpose(self, pe, b, p, kt):
        k, nc, u = self.k, self.k.nc, self.PAIRS * b + p
        if kt == 0:
            pe.wait_ge(*self.probs_ready(u + 1))
        n = NK2 * u + kt
        if not isinstance(u, int) or n >= 2:
            pe.wait_ge(*self.probs_drained(n - 1))
        for r in range(4):
            ins = nc.tensor.transpose(k.probs_ps[:, (NK2 * p + kt) % 2, r * P:(r + 1) * P],
                                      self.probs[:, p % 2, r, kt * P:(kt + 1) * P], k.ident[:])
        ins.then_inc(self.probs_full.sem, 1)

    def t_mix(self, pe, b, p):
        k, nc, u = self.k, self.k.nc, self.PAIRS * b + p
        pe.wait_ge(*self.mixed_drained(u))
        for kt in range(NK2):
            pe.wait_ge(*self.probs_drained(NK2 * u + kt + 1))
            for j in range(2):
                v = self.v[:, p % 2, kt, j * DK2:(j + 1) * DK2] if kt < TPB else \
                    self.mem_v[:, p, j * DK2:(j + 1) * DK2]
                ins = nc.tensor.matmul(k.mixed[j * DK2:(j + 1) * DK2, 0:S], v, self.probs_t[:, kt, j, :],
                                       start=(kt == 0), stop=(kt == NK2 - 1), skip_group_check=True)
        ins.then_inc(self.mixed_full.sem, 1)

    def t_out(self, pe, b, n):
        k, nc = self.k, self.k.nc
        pe.wait_ge(*self.misc_drained(n))
        pe.wait_ge(*self.mixed_drained(self.PAIRS * (b + 1)))
        for t in range(TPB):
            out = k.misc[:, t * P:(t + 1) * P]
            nc.tensor.matmul(out, self.m.row[:, 0, :], self.m.row[:, 2, :], start=True, stop=False)
            for p in range(self.PAIRS):
                ins = nc.tensor.matmul(out, self.mixed_t[:, p, t * P:(t + 1) * P], self.wo[:, p, :], start=False,
                                       stop=(p == self.PAIRS - 1))
        ins.then_inc(self.misc_full.sem, 1)

    def before_unit(self, b, p):
        return (b, p - 1) if p else (b - 1, self.PAIRS - 1)

    def qk_use(self, b, p):
        return 1 if isinstance(b, int) and b == 0 and p == 0 else self.use(*self.before_unit(b, p), "qk")

    def t_batch(self, pe, b, first, last):
        for p in range(self.PAIRS):
            end = p == self.PAIRS - 1
            back = not (first and p == 0)
            for n in range(4):
                self.t_scores(pe, b, p, n)
                if back and 1 <= n < NK2:
                    self.t_transpose(pe, *self.before_unit(b, p), n - 1)
            if not end:
                self.t_qk(pe, b, p + 1, self.use(b, p, "qk"))
            if back:
                self.t_transpose(pe, *self.before_unit(b, p), NK2 - 1)
                self.t_mix(pe, *self.before_unit(b, p))
            if not end:
                self.t_v(pe, p + 1, self.use(b, p, "v"))
            elif not last:
                self.t_xnt(pe, b + 1, self.use(b, p, "xnt"))
                pe.wait_ge(*self.misc_drained(self.use(b, p, "xnt") + 1))
                self.t_qk(pe, b + 1, 0, self.use(b, p, "qk"))
                self.t_v(pe, 0, self.use(b, p, "v"))
            if p == 0 and back:
                self.t_out(pe, b - 1, self.use(b, p, "out"))

    def batches(self, eng, body):
        body(0, True, False)
        with eng.Fori(1, B - 1) as b:
            body(b, False, False)
        body(B - 1, False, True)

    def tensor(self, pe):
        for drained in self.free + [self.scores_drained, self.probs_drained, self.mixed_drained]:
            pe.wait_ge(*drained(0))
        pe.wait_ge(*self.weights_loaded(80))
        self.t_xnt(pe, 0, 0)
        self.t_qk(pe, 0, 0, 1)
        self.t_v(pe, 0, 2)
        self.batches(self.k.nc.tensor, lambda b, first, last: self.t_batch(pe, b, first, last))
        for kt in range(NK2):
            self.t_transpose(pe, B - 1, self.PAIRS - 1, kt)
        self.t_mix(pe, B - 1, self.PAIRS - 1)
        self.t_out(pe, B - 1, 18 * B - 1)


    def v_max(self, dve, b, p):
        k, nc, u = self.k, self.k.nc, self.PAIRS * b + p
        for n in range(4):
            dve.wait_ge(*self.scores_full(4 * u + n + 1))
            nc.vector.tensor_reduce(self.neg_max[:, p % 2, n:n + 1], k.scores[:, n, 0:S + MEM], AX.X, ALU.max,
                                    negate=True).then_inc(self.max_done.sem, 1)

    def v_normalise(self, dve, order, b, p):
        nc, u = self.k.nc, self.PAIRS * b + p
        dve.wait_ge(*self.scores_drained(4 * u + 4))
        if not isinstance(u, int) or u > 0:
            dve.wait_ge(*self.probs_ready(u))
        order.mark(nc.vector.reciprocal(self.rsum[:], self.sum[:, p % 2, :]))
        order.wait()
        for r in range(4):
            ins = nc.vector.tensor_scalar(self.probs[:, p % 2, r, :], self.probs[:, p % 2, r, :], self.rsum[:, r:r + 1],
                                          None, ALU.mult)
        ins.then_inc(self.probs_ready.sem, 1)

    def v_values(self, dve, p, n):
        k, nc = self.k, self.k.nc
        dve.wait_ge(*self.misc_full(n + 1))
        nc.vector.tensor_tensor(self.v[:, p % 2, :, :], k.misc[:, 0:S].rearrange("p (t d) -> p t d", t=TPB),
                                spread(self.v_bias[:, p, :], 1, TPB), ALU.add).then_inc(self.misc_drained.sem, 1)

    def v_out(self, dve, b, n):
        k, nc = self.k, self.k.nc
        dve.wait_ge(*self.misc_full(n + 1))
        x = k.x[:, bass.ds(b * TPB, TPB), :]
        nc.vector.scalar_tensor_tensor(out=x, in0=k.misc[:, 0:S].rearrange("p (t d) -> p t d", t=TPB),
                                       scalar=self.gate, in1=x, op0=ALU.mult, op1=ALU.add)\
            .then_inc(self.misc_drained.sem, 1)

    def v_batch(self, dve, order, b, first, last):
        k = self.k
        for p in range(self.PAIRS):
            end = p == self.PAIRS - 1
            self.v_max(dve, b, p)
            self.v_normalise(dve, order, b, p)
            if not (end and last):
                self.v_values(dve, (p + 1) % self.PAIRS, self.use(b, p, "v"))
            if p == 0 and not first:
                self.v_out(dve, b - 1, self.use(b, p, "out"))
            if p == 2 and not last:
                k.ln_vector_stats(dve, order, k.x[:, bass.ds((b + 1) * TPB, TPB), :], TPB, self.stats, 0)
            if p == 3 and not last:
                k.ln_vector_scale(dve, k.x[:, bass.ds((b + 1) * TPB, TPB), :], TPB, self.rstd, self.normed, b + 2)

    def vector(self, dve, order):
        k = self.k
        dve.wait_ge(*self.before.x_written)
        dve.wait_ge(*self.weights_loaded(80))
        order.wait()
        k.ln_vector_stats(dve, order, k.x[:, 0:TPB, :], TPB, self.stats, 0)
        k.ln_vector_scale(dve, k.x[:, 0:TPB, :], TPB, self.rstd, self.normed, 1)
        self.v_values(dve, 0, 2)
        self.v_batch(dve, order, 0, True, False)
        with k.nc.vector.Fori(1, B - 1) as b, order.turns(b - 1, B - 2, self.PAIRS + 1):
            self.v_batch(dve, order, b, False, False)
        self.v_batch(dve, order, B - 1, False, True)
        self.v_out(dve, B - 1, 18 * B - 1)


    def s_exp(self, act, b, p, n):
        k, nc, u = self.k, self.k.nc, self.PAIRS * b + p
        if n == 0 and (not isinstance(u, int) or u >= 2):
            act.wait_ge(*self.probs_full(NK2 * (u - 1)))
        act.wait_ge(*self.max_done(4 * u + n + 1))
        nc.scalar.activation(self.probs[:, p % 2, n, :], k.scores[:, n, 0:S + MEM], ACT.Exp,
                             bias=self.neg_max[:, p % 2, n:n + 1], accum_out=self.sum[:, p % 2, n:n + 1])\
            .then_inc(self.scores_drained.sem, 1)

    def s_xnt(self, act, n):
        k, nc = self.k, self.k.nc
        act.wait_ge(*self.misc_full(n + 1))
        nc.scalar.activation(self.xnt, k.misc[:, 0:S], ACT.Copy).then_inc(self.misc_drained.sem, 1)

    def s_qk(self, act, p, n):
        k, nc = self.k, self.k.nc
        act.wait_ge(*self.misc_full(n + 1))
        nc.scalar.activation(self.q[:, p % 2, :], k.misc[:, 0:S], ACT.Identity, scale=1.0 / 8,
                             bias=self.bias[:, 2, p:p + 1])
        nc.scalar.activation(self.key[:, p % 2, :], k.misc[:, S:2 * S], ACT.Identity, bias=self.bias[:, 1, p:p + 1])\
            .then_inc(self.misc_drained.sem, 1)

    def s_probs(self, act, b, p, kt):
        k, nc, u = self.k, self.k.nc, self.PAIRS * b + p
        if kt == 0:
            act.wait_ge(*self.mixed_full(u))
        act.wait_ge(*self.probs_full(NK2 * u + kt + 1))
        nc.scalar.activation(self.probs_t[:, kt, :, :].rearrange("p j s -> p (j s)"),
                             k.probs_ps[:, (NK2 * p + kt) % 2, :], ACT.Copy).then_inc(self.probs_drained.sem, 1)

    def s_mix(self, act, b, p):
        k, nc, u = self.k, self.k.nc, self.PAIRS * b + p
        act.wait_ge(*self.mixed_full(u + 1))
        nc.scalar.activation(self.mixed_t[:, p, :], k.mixed[:, 0:S], ACT.Copy).then_inc(self.mixed_drained.sem, 1)

    def s_batch(self, act, b, first, last):
        for p in range(self.PAIRS):
            end = p == self.PAIRS - 1
            back = not (first and p == 0)
            for n in range(4):
                self.s_exp(act, b, p, n)
                if back and n < NK2 - 1:
                    self.s_probs(act, *self.before_unit(b, p), n)
            if not end:
                self.s_qk(act, p + 1, self.use(b, p, "qk"))
            if back:
                self.s_probs(act, *self.before_unit(b, p), NK2 - 1)
                self.s_mix(act, *self.before_unit(b, p))
            if end and not last:
                self.s_xnt(act, self.use(b, p, "xnt"))
                self.s_qk(act, 0, self.use(b, p, "qk"))

    def scalar(self, act, order):
        nc = self.k.nc
        act.wait_ge(*self.weights_loaded(80))
        order.mark(nc.scalar.activation(self.bias[:, 2, :], self.bias[:, 0, :], ACT.Copy, scale=1.0 / 8))
        order.wait()
        self.s_xnt(act, 0)
        self.s_qk(act, 0, 1)
        self.batches(nc.scalar, lambda b, first, last: self.s_batch(act, b, first, last))
        for kt in range(NK2):
            self.s_probs(act, B - 1, self.PAIRS - 1, kt)
        self.s_mix(act, B - 1, self.PAIRS - 1)

    def gpsimd(self, pool, order):
        with self.k.nc.gpsimd.Fori(0, B) as b, order.turns(b, B, 1):
            self.k.ln_pool(pool, order, TPB, self.stats, self.rstd, b + 1)


    def sync(self, sp):
        ins, done = self.k.ins, self.weights_loaded.sem
        sp.wait_ge(*self.weights_free)
        sp.dma_start(self.m.w[:], ins[self.prefix + "w"]).then_inc(done, 16)
        sp.dma_start(self.m.row[:], ins[self.prefix + "row"]).then_inc(done, 16)
        sp.dma_start(self.k.y[:], ins[self.prefix + "memory"]).then_inc(done, 16)
        sp.dma_start(self.v_bias[:], ins[self.prefix + "v_bias"]).then_inc(done, 16)
        sp.dma_start(self.bias[:, 0:2, :], ins[self.prefix + "bias"]).then_inc(done, 16)
        sp.dma_start(self.ctx_t, ins["ctx_t"][:, 0:S]).then_inc(self.ctx_loaded.sem, 16)
        sp.wait_ge(*self.misc_full(self.use(0, self.PAIRS - 2, "v") + 1))
        apart(sp, self.k)
        sp.dma_start(self.ctx_t, ins["ctx_t"][:, S:2 * S]).then_inc(self.ctx_loaded.sem, 16)
        with self.k.nc.sync.Fori(1, B - 1) as b:
            sp.wait_ge(*self.misc_full(self.use(b, self.PAIRS - 2, "v") + 1))
            apart(sp, self.k)
            sp.dma_start(self.ctx_t, ins["ctx_t"][:, bass.ds((b + 1) * S, S)]).then_inc(self.ctx_loaded.sem, 16)


class Normalise:

    def __init__(self, core, before):
        self.k, self.before = core, before
        c = core.count
        self.stats, self.rstd, self.normed = (c(f"ln_{n}", NC) for n in ("stats_done", "rstd_done", "normed"))
        self.x_written = self.normed(NC)

    def tensor(self, pe):
        pass

    def scalar(self, act, order):
        pass

    def sync(self, sp):
        pass

    def vector(self, dve, order):
        k = self.k
        dve.wait_ge(*self.before.x_written)
        order.wait()
        with k.nc.vector.Fori(0, NC) as c, order.turns(c, NC, 1):
            x = k.x[:, bass.ds(c * CH, CH), :]
            k.ln_vector_stats(dve, order, x, CH, self.stats, 0)
            k.ln_vector_scale(dve, x, CH, self.rstd, self.normed, c + 1, out=k.y[:, bass.ds(c * CH, CH), :])

    def gpsimd(self, pool, order):
        with self.k.nc.gpsimd.Fori(0, NC) as c, order.turns(c, NC, 1):
            self.k.ln_pool(pool, order, CH, self.stats, self.rstd, c + 1)


def build(nc, ins, out, stages=10):
    ins = {name: ap for name, ap in ins.items()}
    with ExitStack() as ctx:
        k = Core(nc, ctx, ins)
        orders = {n: ctx.enter_context(nc.semaphore("order_" + n)) for n in ("vector", "scalar", "gpsimd")}
        xg = [k.gates[:, 0, i:i + 1] for i in range(4)]
        fg = [k.gates[:, 1, i:i + 1] for i in range(4)]
        layers = [Setup(k), RowAttention(k, xg[0])]
        m = AttentionMemory(k)
        plan = PLAN(k, m, xg, fg)
        for make in plan[:stages - 1]:
            layers += make(layers[-1])
        last = layers[-1]
        block = ctx.enter_context(nc.Block())

        @block.sync
        def _(sp):
            layers[0].load_first(sp)
            layers[1].sync(sp)
            layers[0].sync(sp)
            for layer in layers[2:]:
                layer.sync(sp)
            sp.wait_ge(*last.x_written)
            sp.dma_start(out.rearrange("(n p) d -> p n d", p=P), k.x[:]).then_inc(k.loaded_stored, 16)
            sp.wait_ge(k.loaded_stored, 16)

        @block.tensor
        def _(pe):
            for name in ("down_full", "mixed_full"):
                nc.tensor.sem_inc(k.signals[name].sem, CREDIT[name])
            for layer in layers:
                layer.tensor(pe)

        @block.vector
        def _(dve):
            order = Order(dve, orders["vector"])
            for name in ("down_drained", "hidden_done"):
                nc.vector.sem_inc(k.signals[name].sem, CREDIT[name])
            for layer in layers:
                layer.vector(dve, order)

        @block.scalar
        def _(act):
            order = Order(act, orders["scalar"])
            for name in ("up_drained", "probs_drained", "mixed_drained"):
                nc.scalar.sem_inc(k.signals[name].sem, CREDIT[name])
            for layer in layers:
                layer.scalar(act, order)

        @block.gpsimd
        def _(pool):
            order = Order(pool, orders["gpsimd"])
            for n, layer in enumerate(layers):
                layer.gpsimd(pool, order)
                if n == 1:
                    m.clear(pool)


def PLAN(k, m, xg, fg):
    return [
        lambda b: [ExpertLayer(k, "cosine", "l0_", fg[0], b)],
        lambda b: [NarrowAttention(k, m, "integer", "l1_", xg[1], b)],
        lambda b: [DenseLayer(k, fg[1], b)],
        lambda b: [WideAttention(k, m, "l2_", xg[2], b)],
        lambda b: [ExpertLayer(k, "softmax", "l2_", fg[2], b)],
        lambda b: [NarrowAttention(k, m, "boolean", "l3x_", xg[3], b)],
        lambda b: [Normalise(k, b)],
        lambda b: [NarrowAttention(k, m, "causal", "l3c_", None, b)],
        lambda b: [ExpertLayer(k, "gated", "l3_", fg[3], b)],
    ]



def stacked(w):
    w = np.asarray(w).reshape(-1, NG, GH, HD)
    out = np.zeros((w.shape[0], NG, GH, Q32), w.dtype)
    for j in range(1, 4):
        out[..., j * HD:(j + 1) * HD] = w
    return out.reshape(w.shape[0], NG, P)


def rows(v):
    return np.broadcast_to(np.asarray(v).reshape(1, -1), (P, np.asarray(v).size))


def arrange(i):
    f = np.float32
    a = {}

    consts = np.zeros((P, N_CONSTS), f)
    consts[:, C_MHALF:C_MHALF + CH] = -0.5
    consts[:, C_HALF:C_HALF + CH] = 0.5
    consts[:, C_E:C_E + CH * (E + 1)] = np.e
    consts[:, C_IOTA:C_IOTA + E] = np.arange(E)
    consts[np.arange(P), C_HEADS + np.arange(P) // HD] = 1
    row = np.arange(P)
    consts[:, C_SPLIT] = -1.0 * (row % Q32 >= 24)
    consts[:, C_SPLIT + 1] = -1.0 * (row % Q32 // HD == 2)
    consts[:, C_SPLIT + 2] = -1.0 * (row >= 64)
    consts[:, C_ONES] = 1.0 * (row % Q32 == 0)
    consts[:, C_TEMP] = np.asarray(i["L0_ffn_temperature"]).reshape(())
    consts[:, C_L1GATE] = np.asarray(i["L1_ffn_gate"]).reshape(())
    consts[:, C_RAWGATES:C_RAWGATES + 4] = rows(i["g_xattn"])
    consts[:, C_RAWGATES + 4:C_RAWGATES + 8] = rows(i["g_ffn"])
    a["consts"] = consts
    a["ident"] = np.eye(P, dtype=f)
    pos = np.arange(S)
    late = np.where(pos[None, :] > pos[:, None], MASKED, 0.0).astype(f)
    a["causal"] = np.stack([late.reshape(TPB, P, S).transpose(1, 0, 2), late.T.reshape(TPB, P, S).transpose(1, 0, 2)], 1)

    a["x"] = i["x"].reshape(-1, D)
    a["x_last"] = i["x"][:, -1, :]
    a["ctx_n"] = i["ctx_1024"].reshape(-1, D)
    a["ctx_t"] = i["ctx_1024"].reshape(-1, D).T
    a["row_w"] = np.stack([i["L0_xattn_Wq"].T, i["L0_xattn_Wk"], i["L0_xattn_Wv"].T, i["L0_xattn_Wo"].T], 1)

    a["l0_sim"], a["l0_wp"] = i["L0_ffn_sim_matrix"], i["L0_ffn_Wp"]
    for p, up, down in (("l0_", "L0_ffn_W1", "L0_ffn_W2"), ("l2_", "L2_ffn_w1", "L2_ffn_w2")):
        a[p + "up"] = i[up].transpose(1, 0, 2)
        a[p + "down"] = i[down].reshape(E, 4, P, D).transpose(2, 0, 1, 3)
    a["l3_up"] = np.concatenate([i["L3_ffn_w1"], i["L3_ffn_w2"]], 2).transpose(1, 0, 2)
    a["l3_down"] = i["L3_ffn_w3"].reshape(E, 2, P, D).transpose(2, 0, 1, 3)
    for p, b1, b2 in (("l0_", "L0_ffn_b1", "L0_ffn_b2"), ("l2_", "L2_ffn_b1", "L2_ffn_b2"), ("l3_", None, None)):
        s = np.zeros((P, N_SMALL), f)
        if b1:
            s[:, 0:E * 4] = i[b1].reshape(E, 4, P).transpose(2, 0, 1).reshape(P, E * 4)
            s[0:E, S_B2:S_B2 + D] = i[b2]
        a[p + "small"] = s
    a["l0_small"][:, S_PROJ:S_PROJ + D] = i["L0_ffn_Wp"].T
    a["l2_small"][:, S_GATE:S_GATE + E] = i["L2_ffn_gate_w"].T
    a["l3_small"][:, S_GATE:S_GATE + E] = i["L3_ffn_gate_w"]
    a["l3_small"][:, S_AFFINE] = i["L3_ffn_ln2_scale"]
    a["l3_small"][:, S_AFFINE + 1] = i["L3_ffn_ln2_shift"]

    fc = i["L1_ffn_w_fc"].reshape(4, P, D).transpose(1, 0, 2).reshape(P, 512)
    a["l1_latent"] = np.stack([fc, i["L1_ffn_w_proj"]], 1)
    a["l1_lora"] = np.concatenate([i["L1_ffn_fast_b"].T, i["L1_ffn_v"], i["L1_ffn_u"].T], 1)
    attention_operands(a, i)
    return {n: np.ascontiguousarray(v) for n, v in a.items()}


def attention_operands(a, i):
    f = np.float32

    def narrow(p, wq, wk, wv, wo, row_biases=None, biases=None, affine=None):
        a[p + "w"] = np.concatenate([stacked(wq).reshape(P, 512), stacked(wk).reshape(P, 512), wv, wo], 1)
        row = np.zeros((1, 3, P), f)
        row[0, 0] = 1
        bias = np.zeros((P, 2 * NG + 2), f)
        if row_biases:
            row[0, 1], row[0, 2] = row_biases
        if biases:
            for n, b in enumerate(biases):
                bias[:, n * NG:(n + 1) * NG] = stacked(b[None])[0].T
            bias[:, NG:2 * NG] += (np.arange(P) % Q32 == 0)[:, None]
        if affine:
            bias[:, 2 * NG], bias[:, 2 * NG + 1] = affine
        a[p + "row"], a[p + "bias"] = row, bias

    narrow("l1_", i["L1_xattn_w_q"].T, i["L1_xattn_w_k"].T, i["L1_xattn_w_v"].T, i["L1_xattn_w_o"].T)
    narrow("l3x_", i["L3_xattn_Wq"], i["L3_xattn_Wk"], i["L3_xattn_Wv"], i["L3_xattn_Wo"],
           (i["L3_xattn_bv"], i["L3_xattn_bo"]), (i["L3_xattn_bq"], i["L3_xattn_bk"]))
    narrow("l3c_", i["L3_ffn_wq"], i["L3_ffn_wk"], i["L3_ffn_wv"], i["L3_ffn_wo"],
           (np.zeros(D, f), i["L3_ffn_bo"]), None, (i["L3_ffn_ln1_scale"], i["L3_ffn_ln1_shift"]))

    def by_pair(v):
        return np.asarray(v).reshape(H // 2, P, -1).transpose(1, 0, 2)

    a["l2_w"] = np.concatenate([i["L2_xattn_wq_w"], i["L2_xattn_wk_w"], i["L2_xattn_wv_w"],
                                by_pair(i["L2_xattn_wo_w"]).reshape(P, -1)], 1)
    a["l2_row"] = np.stack([np.ones(P, f), np.zeros(P, f), i["L2_xattn_wo_b"]])[None]
    a["l2_bias"] = np.stack([by_pair(i["L2_xattn_wq_b"])[..., 0], by_pair(i["L2_xattn_wk_b"])[..., 0]], 1)
    a["l2_v_bias"] = rows(i["L2_xattn_wv_b"]).reshape(P, H // 2, P)
    mem_k, mem_v = i["L2_xattn_mk"].reshape(MEM, -1), i["L2_xattn_mv"].reshape(MEM, -1)
    a["l2_memory"] = np.concatenate([by_pair(mem_k.T), mem_v.reshape(MEM, H // 2, P)], 1)
    for p, m in (("l1_", i["mask_BxSxS2_ik1"]), ("l3x_", i["mask_Bx1xSxS2_bk1"][:, 0])):
        both = np.stack([m, m.transpose(0, 2, 1)], 1)
        a[p + "mask"] = both.reshape(B, 2, TPB, P, S).transpose(0, 3, 1, 2, 4).reshape(B * P, 2 * TPB * S)


def kernel(**inputs):
    import concourse.bacc as _bacc
    from concourse.bass_utils import run_bass_kernel_spmd as _run

    nc = _bacc.Bacc("TRN2", target_bir_lowering=False, num_devices=1)
    arrays, ins = {}, {}
    for name, a in arrange({n: np.asarray(v) for n, v in inputs.items()}).items():
        arrays["in_" + name] = a
        ins[name] = nc.dram_tensor("in_" + name, a.shape, mybir.dt.from_np(a.dtype), kind="ExternalInput").ap()
    out = nc.dram_tensor("out_x", (B * S, D), F32, kind="ExternalOutput").ap()
    build(nc, ins, out)
    r = _run(nc, [arrays], core_ids=[0])
    return r.results[0]["out_x"].reshape(B, S, D)
```
